# Optimizing a Trainium2 kernel written in Bass

```python
import numpy as np
import jax
import jax.numpy as jnp

def _softmax(x, axis=-1):
    return jax.nn.softmax(x, axis=axis)

def _gelu(x):
    return jax.nn.gelu(x, approximate=True)

def _silu(x):
    return jax.nn.silu(x)

def _sigmoid(x):
    return jax.nn.sigmoid(x)

def _layernorm(x, axis=-1, eps=1e-05):
    m = jnp.mean(x, axis=axis, keepdims=True)
    v = jnp.var(x, axis=axis, keepdims=True)
    return (x - m) / jnp.sqrt(v + eps)

def _scatter_add(tgt, idx, src, axis=0):
    return tgt.at[idx].add(src)

def _segment_sum(src, seg, n):
    return jax.ops.segment_sum(src, seg, n)
kernel_name = 'mk_hybrid_d1_jaxref_r8_493cba'

def setup_inputs(seed: int=0):
    np.random.seed(seed)
    _w = jnp.asarray

    def _L0_attn_a_setup():
        import jax, jax.numpy as jnp
        import numpy as np
        import math
        HIDDEN = 512
        NUM_HEADS = 32
        HEAD_DIM = HIDDEN // NUM_HEADS
        SCALE = 1.0 / HEAD_DIM

        def _alibi_slopes(n_heads: int) -> np.ndarray:
            cp2 = 2 ** math.floor(math.log2(n_heads))
            base = 2 ** (-2 ** (-(math.log2(cp2) - 3)))
            slopes = base ** np.arange(1, cp2 + 1, dtype=np.float32)
            if cp2 != n_heads:
                extra_base = 2 ** (-2 ** (-(math.log2(2 * cp2) - 3)))
                n_rem = min(cp2, n_heads - cp2)
                extra = extra_base ** np.arange(1, 1 + 2 * n_rem, 2, dtype=np.float32)
                slopes = np.concatenate([slopes, extra])
            return slopes.astype(np.float32)
        key = jax.random.key(seed)
        k1, k2, k3, k4, k5 = jax.random.split(key, 5)
        B, S = (2, 256)
        return {'hidden_states': jax.random.normal(k1, (B, S, HIDDEN), dtype=jnp.float32), 'w_attn': jax.random.normal(k2, (HIDDEN, 3 * HIDDEN), dtype=jnp.float32) * 0.02, 'b_attn': jnp.zeros((3 * HIDDEN,), dtype=jnp.float32), 'w_proj': jax.random.normal(k3, (HIDDEN, HIDDEN), dtype=jnp.float32) * 0.02, 'b_proj': jnp.zeros((HIDDEN,), dtype=jnp.float32)}
    _L0_attn_a_in = _L0_attn_a_setup()

    def _L0_attn_b_setup():
        import jax, jax.numpy as jnp
        import numpy as np
        K_FACTOR = 0.5
        key = jax.random.key(seed)
        k1, k2, k3, k4 = jax.random.split(key, 4)
        B, S, H, I = (1, 256, 512, 1376)
        x = jax.random.normal(k1, (B, S, H), dtype=jnp.float32)
        w_gate = jax.random.normal(k2, (I, H), dtype=jnp.float32) * 0.02
        w_up = jax.random.normal(k3, (I, H), dtype=jnp.float32) * 0.02
        w_down = jax.random.normal(k4, (H, I), dtype=jnp.float32) * 0.02
        return {'x': x, 'w_gate': w_gate, 'w_up': w_up, 'w_down': w_down}
    _L0_attn_b_in = _L0_attn_b_setup()

    def _L0_ffn_setup():
        import jax, jax.numpy as jnp
        import numpy as np
        B, S, D = (4, 256, 512)
        NUM_EXPERTS, TOP_K = (3, 2)

        def _expert_outputs(h, w1, b1, w2, b2):
            pre = jnp.einsum('bsd,edf->ebsf', h, w1) + b1[:, None, None, :]
            act = jnp.stack([jnp.tanh(pre[0]), jax.nn.gelu(pre[1], approximate=False), jax.nn.silu(pre[2])])
            return jnp.einsum('ebsf,efd->ebsd', act, w2) + b2[:, None, None, :]
        key = jax.random.key(seed)
        ks = jax.random.split(key, 8)
        scale_in = 1.0 / np.sqrt(D)
        scale_gate = 1.0 / np.sqrt(D + 1)
        return {'h': jax.random.normal(ks[0], (B, S, D), dtype=jnp.float32), 'gate_w': jax.random.uniform(ks[1], (D + 1, NUM_EXPERTS), minval=-scale_gate, maxval=scale_gate, dtype=jnp.float32), 'gate_b': jnp.zeros((NUM_EXPERTS,), dtype=jnp.float32), 'w1': jax.random.uniform(ks[2], (NUM_EXPERTS, D, D), minval=-scale_in, maxval=scale_in, dtype=jnp.float32), 'b1': jnp.zeros((NUM_EXPERTS, D), dtype=jnp.float32), 'w2': jax.random.uniform(ks[3], (NUM_EXPERTS, D, D), minval=-scale_in, maxval=scale_in, dtype=jnp.float32), 'b2': jnp.zeros((NUM_EXPERTS, D), dtype=jnp.float32)}
    _L0_ffn_in = _L0_ffn_setup()
    _d = {'L0_attn_a_hidden_states': _L0_attn_a_in['hidden_states'], 'L0_attn_a_w_attn': _L0_attn_a_in['w_attn'], 'L0_attn_a_b_attn': _L0_attn_a_in['b_attn'], 'L0_attn_a_w_proj': _L0_attn_a_in['w_proj'], 'L0_attn_a_b_proj': _L0_attn_a_in['b_proj'], 'L0_attn_b_w_gate': _L0_attn_b_in['w_gate'], 'L0_attn_b_w_up': _L0_attn_b_in['w_up'], 'L0_attn_b_w_down': _L0_attn_b_in['w_down'], 'L0_ffn_gate_w': _L0_ffn_in['gate_w'], 'L0_ffn_gate_b': _L0_ffn_in['gate_b'], 'L0_ffn_w1': _L0_ffn_in['w1'], 'L0_ffn_b1': _L0_ffn_in['b1'], 'L0_ffn_w2': _L0_ffn_in['w2'], 'L0_ffn_b2': _L0_ffn_in['b2']}
    _x0 = _d['L0_attn_a_hidden_states']
    _d['L0_attn_a_hidden_states'] = jax.random.normal(jax.random.fold_in(jax.random.key(seed), 1), (4, 256, 512), dtype=_x0.dtype)
    del _x0
    return _d

def reference(L0_attn_a_hidden_states, L0_attn_a_w_attn, L0_attn_a_b_attn, L0_attn_a_w_proj, L0_attn_a_b_proj, L0_attn_b_w_gate, L0_attn_b_w_up, L0_attn_b_w_down, L0_ffn_gate_w, L0_ffn_gate_b, L0_ffn_w1, L0_ffn_b1, L0_ffn_w2, L0_ffn_b2):

    def _L0_attn_a_ref(hidden_states, w_attn, b_attn, w_proj, b_proj):
        import jax, jax.numpy as jnp
        import numpy as np
        import math
        HIDDEN = 512
        NUM_HEADS = 32
        HEAD_DIM = HIDDEN // NUM_HEADS
        SCALE = 1.0 / HEAD_DIM

        def _alibi_slopes(n_heads: int) -> np.ndarray:
            cp2 = 2 ** math.floor(math.log2(n_heads))
            base = 2 ** (-2 ** (-(math.log2(cp2) - 3)))
            slopes = base ** np.arange(1, cp2 + 1, dtype=np.float32)
            if cp2 != n_heads:
                extra_base = 2 ** (-2 ** (-(math.log2(2 * cp2) - 3)))
                n_rem = min(cp2, n_heads - cp2)
                extra = extra_base ** np.arange(1, 1 + 2 * n_rem, 2, dtype=np.float32)
                slopes = np.concatenate([slopes, extra])
            return slopes.astype(np.float32)
        B, S, _ = hidden_states.shape
        H, D = (NUM_HEADS, HEAD_DIM)
        qkv = hidden_states @ w_attn + b_attn
        q, k, v = jnp.split(qkv, 3, axis=-1)
        q = q.reshape(B, S, H, D)
        k = k.reshape(B, S, H, D)
        v = v.reshape(B, S, H, D)
        scores = jnp.einsum('bqhd,bkhd->bhqk', q, k) * SCALE
        slopes = jnp.asarray(_alibi_slopes(H))
        pos = jnp.arange(S)
        rel = pos[None, :] - pos[:, None]
        bias = slopes[:, None, None] * rel[None, :, :]
        causal = rel <= 0
        scores = jnp.where(causal[None, None], scores + bias[None], -jnp.inf)
        attn = jax.nn.softmax(scores, axis=-1)
        out = jnp.einsum('bhqk,bkhd->bqhd', attn, v).reshape(B, S, HIDDEN)
        return out @ w_proj + b_proj

    def _L0_attn_b_ref(x, w_gate, w_up, w_down):
        import jax, jax.numpy as jnp
        import numpy as np
        K_FACTOR = 0.5
        s = jax.nn.silu(jnp.einsum('bsh,ih->bsi', x, w_gate))
        B, S, I = s.shape
        k = int(K_FACTOR * I)
        _, idx = jax.lax.top_k(-jnp.abs(s), k)
        flat = s.reshape(B * S, I)
        rows = jnp.arange(B * S)[:, None]
        flat = flat.at[rows, idx.reshape(B * S, k)].set(0.0)
        s = flat.reshape(B, S, I)
        s = s * jnp.einsum('bsh,ih->bsi', x, w_up)
        return jnp.einsum('bsi,hi->bsh', s, w_down)

    def _L0_ffn_ref(h, gate_w, gate_b, w1, b1, w2, b2):
        import jax, jax.numpy as jnp
        import numpy as np
        B, S, D = (4, 256, 512)
        NUM_EXPERTS, TOP_K = (3, 2)

        def _expert_outputs(h, w1, b1, w2, b2):
            pre = jnp.einsum('bsd,edf->ebsf', h, w1) + b1[:, None, None, :]
            act = jnp.stack([jnp.tanh(pre[0]), jax.nn.gelu(pre[1], approximate=False), jax.nn.silu(pre[2])])
            return jnp.einsum('ebsf,efd->ebsd', act, w2) + b2[:, None, None, :]
        b, s, d = h.shape
        vision_len = int(s * 0.3)
        text_strength = jnp.mean(jnp.abs(h[:, vision_len:, :]), axis=(1, 2), keepdims=True)
        vision_strength = jnp.mean(jnp.abs(h[:, :vision_len, :]), axis=(1, 2), keepdims=True)
        modality_ratio = text_strength / (vision_strength + 1e-08)
        modality_ratio = jnp.broadcast_to(modality_ratio, (b, s, 1))
        router_input = jnp.concatenate([h, modality_ratio], axis=-1)
        gate_logits = router_input @ gate_w + gate_b
        gate_scores = jax.nn.softmax(gate_logits, axis=-1)
        top_val, top_idx = jax.lax.top_k(gate_scores, TOP_K)
        top_val = top_val / (jnp.sum(top_val, axis=-1, keepdims=True) + 1e-08)
        expert_out = _expert_outputs(h, w1, b1, w2, b2)
        moe_out = jnp.zeros_like(h)
        batch_idx = jnp.arange(b)
        for i in range(TOP_K):
            j = top_idx[:, 0, i]
            out_i = expert_out[j, batch_idx]
            moe_out = moe_out + top_val[..., i:i + 1] * out_i
        return moe_out
    x = L0_attn_a_hidden_states
    x = x + _L0_attn_a_ref(_layernorm(x, axis=-1), L0_attn_a_w_attn, L0_attn_a_b_attn, L0_attn_a_w_proj, L0_attn_a_b_proj)
    x = x + _L0_ffn_ref(_layernorm(x, axis=-1), L0_ffn_gate_w, L0_ffn_gate_b, L0_ffn_w1, L0_ffn_b1, L0_ffn_w2, L0_ffn_b2)
    x = x + _L0_attn_b_ref(_layernorm(x, axis=-1), L0_attn_b_w_gate, L0_attn_b_w_up, L0_attn_b_w_down)
    x = x + _L0_ffn_ref(_layernorm(x, axis=-1), L0_ffn_gate_w, L0_ffn_gate_b, L0_ffn_w1, L0_ffn_b1, L0_ffn_w2, L0_ffn_b2)
    return x

_drawn_inputs = setup_inputs


def setup_inputs(seed=0):
    import zlib

    import numpy as np

    out = dict(_drawn_inputs(seed))
    spreads = {'L0_attn_a_b_attn': (0.0, 0.1),
     'L0_attn_a_b_proj': (0.0, 0.1),
     'L0_ffn_gate_b': (0.0, 0.1),
     'L0_ffn_b1': (0.0, 0.1),
     'L0_ffn_b2': (0.0, 0.1)}
    factors = {}
    for name, (base, spread) in spreads.items():
        noise = np.random.default_rng([zlib.crc32(name.encode()), seed]).standard_normal(out[name].shape)
        drawn = base * np.exp(spread * noise) if base else spread * noise
        out[name] = jnp.asarray(drawn.astype(out[name].dtype))
    for name, factor in factors.items():
        out[name] = (out[name] * factor).astype(out[name].dtype)
    return out
```

```python
from contextlib import ExitStack

import numpy as np

import concourse.bass as bass
from concourse import mybir

F32 = mybir.dt.float32
BF16 = mybir.dt.bfloat16
U16 = mybir.dt.uint16
I32 = mybir.dt.int32
ALU = mybir.AluOpType
ACT = mybir.ActivationFunctionType
AX = mybir.AxisListType

P = 128
NEG = -1.0e30
EPS = 1e-5

TERMS = [(0, 0), (0, 1), (1, 0), (1, 1), (0, 2), (2, 0)]
BIAS_PARTS = 4
MAX_PARTS = 3


class Step:

    def __init__(self, var, mul, add):
        self.var, self.mul, self.add = var, mul, add

    def index(self):
        return self.var * self.mul + self.add


class Signal:

    def __init__(self, sem, per, credit=0):
        self.sem, self.per, self.credit = sem, per, credit
        self.waited = Signal.waits

    def count(self, step, k):
        if isinstance(step, Step):
            return step.var * (step.mul * self.per) + (step.add * self.per + k + self.credit)
        return step * self.per + (k + self.credit)


def need(eng, signal, step, k):
    if isinstance(step, int) and signal.count(step, k) <= 0:
        return
    eng.wait_ge(signal.sem, signal.count(step, k))


def need_apart(eng, signal, step, k):
    need(eng, signal, step, k)
    if not isinstance(step, int):
        eng.sem_inc(signal.waited, 1)


def shift(step, n):
    return Step(step.var, step.mul, step.add + n) if isinstance(step, Step) else step + n


class NormSignals:

    def __init__(self, sig, name):
        self.stat = sig(name + "_stat", 2)
        self.rstd = sig(name + "_rstd", 2)
        self.rows = sig(name + "_rows", 1)


class RouteSignals:

    def __init__(self, sig, name, E):
        self.logit = sig(name + "_logit", E, credit=1)
        self.mag = sig(name + "_mag", 1, credit=1)
        self.sums = sig(name + "_sums", 1)
        self.shifted = sig(name + "_shifted", 1)
        self.exp = sig(name + "_exp", 1)
        self.rank = sig(name + "_rank", 1)
        self.spread = sig(name + "_spread", 1)
        self.chain = sig(name + "_chain", 0)
        self.coef = sig(name + "_coef", 1)


class FFNSignals:

    def __init__(self, sig, name, E):
        self.row = sig(name + "_row", 1)
        self.hT_ps = sig(name + "_hT_ps", 1)
        self.hT = sig(name + "_hT", 1)
        self.pre = sig(name + "_pre", 2)
        self.fun = sig(name + "_fun", 6)
        self.mix = sig(name + "_mix", 8)
        self.aT_ps = sig(name + "_aT_ps", 2)
        self.aT = sig(name + "_aT", 2)
        self.y_ps = sig(name + "_y_ps", 1)
        self.y_add = sig(name + "_y_add", 1, credit=1)
        self.b2_add = sig(name + "_b2_add", E)


class MLPSignals:

    def __init__(self, sig, picks, slow):
        self.turned = sig("mlp_turned", 1)
        self.kept = sig("mlp_kept", 1)
        self.row = sig("mlp_row", 1)
        self.hT_ps = sig("mlp_hT_ps", 1)
        self.hT = sig("mlp_hT", 1)
        self.gate = sig("mlp_gate", 1)
        self.up = sig("mlp_up", 1)
        self.silu = sig("mlp_silu", 1)
        self.size = sig("mlp_size", 1)
        self.pick = sig("mlp_pick", picks)
        self.check = sig("mlp_check", 1)
        self.prod = sig("mlp_prod", 3)
        self.slow = sig("mlp_slow", slow)
        self.prodT_ps = sig("mlp_prodT_ps", 3)
        self.prodT = sig("mlp_prodT", 4)
        self.y_ps = sig("mlp_y_ps", 1)
        self.y_add = sig("mlp_y_add", 1, credit=1)


def index(step):
    return step.index() if isinstance(step, Step) else step


def tile_step(b, j, tiles):
    return b * tiles + j if isinstance(b, int) else Step(b, tiles, j)


def alibi_slopes(n):
    base = 2 ** (-2 ** (-(np.log2(n) - 3)))
    return (base ** np.arange(1, n + 1, dtype=np.float32)).astype(np.float32)


def bf16_parts(a, n):
    out = []
    for _ in range(n):
        top = (a.astype(np.float32).view(np.uint32) & 0xFFFF0000).view(np.float32)
        out.append((top.view(np.uint32) >> 16).astype(np.uint16))
        a = a - top.astype(np.float64)
    return out


def alibi_rows(H, S):
    ramp = alibi_slopes(H).astype(np.float64)[:, None] * np.arange(S, dtype=np.float64)[None, :]
    one = np.full((H, S), 0x3F80, np.uint16)
    k_rows, q_rows = [], []
    for kp, qp in zip(bf16_parts(ramp, BIAS_PARTS), bf16_parts(-ramp, BIAS_PARTS)):
        k_rows += [kp, one]
        q_rows += [one, qp]
    k_rows += [one] * MAX_PARTS
    return np.stack(k_rows), np.stack(q_rows)


def build(nc, x_in, w_attn, b_attn, w_proj, b_proj, w_gate, w_up, w_down,
          gate_w, gate_b, w1_in, b1_in, w2_in, b2_in, k_alibi, q_alibi, out, stop=None):
    B, S, D = x_in.shape
    H = k_alibi.shape[1]
    HD = D // H
    KC = D // P
    T = B * S // P
    TB = S // P
    E = w1_in.shape[0]
    I = w_gate.shape[0]
    IC = (I + P - 1) // P
    G = 4
    NG = H // G
    HT = D // P
    H8 = P // HD
    TROWS = len(TERMS) * HD
    SROWS = TROWS + 2 * BIAS_PARTS
    MROWS = SROWS + MAX_PARTS
    SCALE = 1.0 / HD
    KEEP = I - I // 2
    BITS = 31
    PROBES, FIRST_GUESS, STEP, AIM = 4, 0.78, 0.0011, KEEP - 8
    VISION = int(S * 0.3)
    assert TB == 2 and D == 512

    with ExitStack() as ctx:
        def sem(name):
            return ctx.enter_context(nc.semaphore(name))

        def sig(name, per, credit=0):
            return Signal(sem(name), per, credit)

        at = [32 * ((nc.sbuf_base + 31) // 32)]

        def sb(name, shape, dt, offset=None):
            size = {F32: 4, I32: 4, BF16: 2, U16: 2}[dt]
            n = size
            for s in shape[1:]:
                n *= s
            if offset is None:
                offset = at[0]
                at[0] += 32 * ((n + 31) // 32)
                assert at[0] <= nc.sbuf_usable_end, (name, at[0])
            return nc.alloc_sbuf_tensor_at(name, shape, dt, offset=offset)

        x_sb = sb("x_sb", [P, T, D], F32)
        h_sb_at = at[0]
        h_sb = sb("h_sb", [P, TB, D], F32)
        ident = sb("ident", [P, P], F32)
        ident16 = sb("ident16", [P, P], BF16)
        ones16 = sb("ones16", [P, P], BF16)
        neg_half = sb("neg_half", [P, TB], F32)
        stats = sb("stats", [P, TB, 6], F32)
        moments = sb("moments", [P, TB, 2], F32)
        spread = sb("spread", [P, TB], F32)
        rstd = sb("rstd", [P, TB], F32)
        NBIAS = 3 * D + D + E * D
        bias3 = sb("bias3", [P, NBIAS], BF16)
        B_ATTN, B_PROJ, B_1 = 0, 3 * D, 4 * D

        h_all = sb("h_all", [P, T, D], F32)
        ln_stats = sb("ln_stats", [P, 6], F32)
        ln_moments = sb("ln_moments", [P, 2], F32)
        ln_spread = sb("ln_spread", [P, 1], F32)
        ln_rstd = sb("ln_rstd", [P, 1], F32)
        logits = sb("logits", [P, T, E], F32)
        abs_sum = sb("abs_sum", [P, T], F32)
        gate_row = sb("gate_row", [P, (D + 1) * E], F32)
        gate_bias = sb("gate_bias", [P, E], F32)
        b2_row = sb("b2_row", [P, E, D], F32)
        junk = sb("junk", [P, D], F32)
        abs_junk = sb("abs_junk", [P, D], BF16)
        vision = sb("vision", [P, P], F32)
        text = sb("text", [P, P], F32)
        ones32 = sb("ones32", [P, P], F32)
        first_row = sb("first_row", [P, P], BF16)
        coef = sb("coef", [P, 2, T, E], F32)
        coef_b2 = sb("coef_b2", [P, T, E], F32)
        experts = sb("experts", [P, 2, B], I32)
        tiny = sb("tiny", [P, 21, T * E], F32)
        bits = sb("bits", [P, BITS], I32)
        cut_at = sb("cut_at", [P, 1], I32)
        cut_try = sb("cut_try", [P, 1], I32)
        cut_add = sb("cut_add", [P, 1], I32)
        cut_count = sb("cut_count", [P, 1], F32)
        surplus = sb("surplus", [P, 1], F32)
        guess = sb("guess", [P, 1], F32)
        guess_step = sb("guess_step", [P, 1], F32)
        threshold = sb("threshold", [P, 1], F32)
        size_sum = sb("size_sum", [P, 1], F32)
        short = sb("short", [P, 1], F32)
        failed = sb("failed", [P, 1], F32)
        failures = sb("failures", [P, 1], I32)
        ladder = sb("ladder", [P, 1 + 2 * 8], F32)
        numbers = sb("numbers", [P, 1 + 2 * 8], F32)
        pickout = sb("pickout", [P, 1 + 2 * 8], F32)

        arena = at[0]
        wqkv = sb("wqkv", [P, KC, 3 * D], F32)
        qk_tok = sb("qk_tok", [P, TB, 2 * D], F32)
        parts = sb("parts", [P, 2, 3, HT, S], BF16)
        resid = sb("resid", [P, 2, 2 * S], F32)
        gathered_end = at[0]
        wproj = sb("wproj", [P, KC, D], F32)
        actT = sb("actT", [P, KC, S], F32)
        stack_at = at[0]
        qst = sb("qst", [P, H, S], BF16)
        kst = sb("kst", [P, H, S], BF16)
        values_at = at[0]
        v_stage = sb("v_stage", [P, TB, D], F32)
        v_ones = sb("v_ones", [P, TB, H, 2 * HD], F32)
        probs_at = at[0]
        probsT = sb("probsT", [P, 2, 3 * D], F32)
        outT = sb("outT", [P, 2, S], F32)
        o_tok = sb("o_tok", [P, TB, D], F32)
        rden = sb("rden", [P, 2, TB * G], F32)
        maskS = sb("maskS", [P, P], BF16)
        maskT = sb("maskT", [P, P], BF16)
        nmax = sb("nmax", [P, TB, H], F32)
        nmax_r = sb("nmax_r", [P, TB, H], F32)
        nmax_p = sb("nmax_p", [P, TB, MAX_PARTS, H], BF16)
        nmaxT = sb("nmaxT", [P, S], BF16)

        b_raw = sb("b_raw", [P, NBIAS], F32)
        b_p1 = sb("b_p1", [P, NBIAS], BF16, probs_at)
        b_p2 = sb("b_p2", [P, NBIAS], BF16, probs_at + 2 * NBIAS)

        at[0] = arena
        w1_sb = sb("w1_sb", [P, E, KC, D], F32)
        w2_sb = sb("w2_sb", [P, E, KC, D], F32)
        assert at[0] <= gathered_end
        ffn_at = at[0]
        h_cur = sb("h_cur", [P, 2, D], F32)
        hT = sb("hT", [P, 2, KC, P], F32, h_sb_at)
        funs = sb("funs", [P, 2, 3, D], F32)
        act_tok = sb("act_tok", [P, 2, 2, D], F32)
        aT = sb("aT", [P, 2, KC, P], F32)
        weights_at = max(at[0], ffn_at + 8 * D + 14 * I + 4 * IC * P + 128)
        weights_at = 32 * ((weights_at + 31) // 32)
        region = [weights_at + i * 4 * IC * D for i in range(3)]
        assert weights_at + 12 * IC * D <= nc.sbuf_usable_end
        wgT = sb("wgT", [P, KC, I], F32, region[0])
        wuT = sb("wuT", [P, KC, I], F32, region[1])
        wdT = sb("wdT", [P, IC, D], F32, region[2])
        gate_raw = sb("gate_raw", [P, IC, D], F32, region[1])
        up_raw = sb("up_raw", [P, IC, D], F32, region[2])
        down_raw = sb("down_raw", [P, KC, I], F32, arena)
        assert 4 * KC * I <= 4 * E * KC * D
        at[0] = ffn_at + 8 * D
        mlp_s = sb("mlp_s", [P, I], F32)
        mlp_size = sb("mlp_size", [P, I], F32)
        mlp_prod = sb("mlp_prod", [P, I], F32)
        mlp_flag = sb("mlp_flag", [P, I], BF16)
        at_prodT = max(at[0], 0)
        prodT = sb("prodT", [P, IC, P], F32, at_prodT)
        assert at_prodT + 4 * IC * P <= region[0], (at_prodT + 4 * IC * P, region[0])

        ps = ctx.enter_context(nc.psum_tensor("ps", [P, 8, 512], F32))

        x_first, x_rest = sem("x_first"), sem("x_rest")
        wqkv_in, wproj_in, alibi_in, bias_in = sem("wqkv_in"), sem("wproj_in"), sem("alibi_in"), sem("bias_in")
        consts, ident_ok, bits_set = sem("consts"), sem("ident_ok"), sem("bits_set")
        bias_cut, bias_zero, bias_in2 = sem("bias_cut"), sem("bias_zero"), sem("bias_in2")
        Signal.waits = sem("waits")
        stat = sig("stat", 2 * TB)
        rstd_ok = sig("rstd_ok", 2)
        h_ok = sig("h_ok", TB)
        hT_ps = sig("hT_ps", TB)
        hT_ok = sig("hT_ok", TB)
        qkv_ps = sig("qkv_ps", 3 * TB)
        qv_out = sig("qv_out", 2 * TB)
        k_out = sig("k_out", TB)
        tr_ps = sig("tr_ps", 4)
        part1 = sig("part1", 4)
        res1 = sig("res1", 4)
        part2 = sig("part2", 4)
        part3 = sig("part3", 4)
        cuts_out = sig("cuts_out", 32)
        scat = [sig(f"scat{half}", 16 * 2 * len(TERMS)) for half in range(2)]
        GHALF = NG // 2
        v_copy = sig("v_copy", 1)
        s_ps = sig("s_ps", NG)
        max_ok = sig("max_ok", 2 * NG)
        nm_cut = sig("nm_cut", 4)
        nmT_ps = sig("nmT_ps", 1)
        nmT_ok = sig("nmT_ok", 1)
        nm_in = sig("nm_in", 16 * MAX_PARTS)
        sT_ps = sig("sT_ps", NG)
        exp_ok = sig("exp_ok", NG)
        pv_ps = sig("pv_ps", NG)
        outT_ok = sig("outT_ok", NG)
        oTr_ps = sig("oTr_ps", NG)
        rden_ok = sig("rden_ok", NG)
        norm_ok = sig("norm_ok", NG)
        oT_ps = sig("oT_ps", TB)
        oT_ok = sig("oT_ok", TB)
        y_ps = sig("y_ps", TB)
        x_add = sig("x_add", TB, credit=TB)

        norm2, norm3, norm4 = NormSignals(sig, "norm2"), NormSignals(sig, "norm3"), NormSignals(sig, "norm4")
        route1, route2 = RouteSignals(sig, "route1", E), RouteSignals(sig, "route2", E)
        ffn1, ffn2 = FFNSignals(sig, "ffn1", E), FFNSignals(sig, "ffn2", E)
        SLOW = 1 + 4 * BITS + 8
        PICKS = 1 + 3 * (PROBES - 1) + 10
        mlp = MLPSignals(sig, PICKS, SLOW)
        gate_in, w12_in = sem("gate_in"), sem("w12_in")
        mlp_w_in, down_in, w12_in2 = sem("mlp_w_in"), sem("down_in"), sem("w12_in2")
        out_done = sem("out_done")

        cuts = nc.dram_tensor("cuts", (2, 3, D, S), BF16, kind="Internal").ap()
        x_v = x_in.rearrange("b (j p) d -> p (b j) d", p=P)
        out_v = out.rearrange("b (j p) d -> p (b j) d", p=P)

        gate_v = gate_row[:, :].rearrange("p (d e) -> p d e", e=E)
        bias1 = bias3[:, B_1:B_1 + E * D].rearrange("p (e n) -> p e n", e=E)
        slot = [ps[:, 0:3, :], ps[:, 3:6, :]]
        work = [ps[:, 6, :], ps[:, 7, :]]

        gate_ps = ps[:, 0:3, :].rearrange("p b n -> p (b n)")[:, 0:I]
        check_ps = ps[0:1, 7, 0:1]
        up_ps = ps[:, 3:6, :].rearrange("p b n -> p (b n)")[:, 0:I]

        ROW_BANK, CHECK_BANK, PROD_BANK, Y_BANK = 6, 7, (6, 7, 6), 7

        block = ctx.enter_context(nc.Block())

        @block.sync
        def _(sp):
            sp.dma_start(x_sb[:, 0:TB, :], x_v[:, 0:TB, :]).then_inc(x_first, 16)
            wa = w_attn.rearrange("(c p) n -> p c n", p=P)
            for c in range(KC):
                sp.dma_start(wqkv[:, c, :], wa[:, c, :]).then_inc(wqkv_in, 16)
            sp.dma_start(x_sb[:, TB:T, :], x_v[:, TB:T, :]).then_inc(x_rest, 16)
            sp.dma_start(kst[TROWS:MROWS, :, :].bitcast(U16), k_alibi).then_inc(alibi_in, 16)
            sp.dma_start(qst[TROWS:SROWS, :, :].bitcast(U16), q_alibi).then_inc(alibi_in, 16)
            sp.dma_start(gate_row[:, :], gate_w.rearrange("d e -> (d e)").partition_broadcast(P)).then_inc(gate_in, 16)
            sp.dma_start(gate_bias[:, :], gate_b.partition_broadcast(P)).then_inc(gate_in, 16)
            sp.dma_start(b2_row[:, :, :].rearrange("p e n -> p (e n)"),
                         b2_in.rearrange("e n -> (e n)").partition_broadcast(P)).then_inc(gate_in, 16)
            sp.dma_start(wproj[:, :, :], w_proj.rearrange("(c p) n -> p c n", p=P)).then_inc(wproj_in, 16)

            def gather(b, before):
                for side in range(2):
                    need(sp, part3, b, 2 * side + 2)
                    sp.dma_start(cuts[side].rearrange("m (g p) t -> p (m g) t", p=P),
                                 parts[:, side, :, :, :].rearrange("p m g t -> p (m g) t")).then_inc(cuts_out.sem, 16)
                need(sp, cuts_out, b, 32)
                for half in range(2):
                    need(sp, sT_ps, before, (half + 1) * GHALF)
                    hs = slice(half * H // 2, (half + 1) * H // 2)
                    for side, stack in enumerate((qst, kst)):
                        for t, term in enumerate(TERMS):
                            sp.dma_start(
                                stack[HD * t:HD * t + HD, hs, :],
                                cuts[side, term[1 - side]].rearrange("(h d) t -> d h t", d=HD)[:, hs, :],
                            ).then_inc(scat[half].sem, 16)

            gather(0, -1)
            with sp.Fori(0, B - 1) as b:
                gather(b + 1, b)

            need(sp, qkv_ps, B - 1, 3 * TB)
            for half in range(2):
                need(sp, scat[half], B - 1, scat[half].per)
            for e in range(E):
                sp.dma_start(w1_sb[:, e], w1_in[e].rearrange("(c p) n -> p c n", p=P)).then_inc(w12_in, 16)
            for e in range(E):
                sp.dma_start(w2_sb[:, e], w2_in[e].rearrange("(c p) n -> p c n", p=P)).then_inc(w12_in, 16)

            need(sp, y_ps, B - 1, TB)
            full = I // P * P
            for raw, w in ((gate_raw, w_gate), (up_raw, w_up)):
                sp.dma_start(raw[:, 0:I // P, :], w[0:full].rearrange("(c p) n -> p c n", p=P)).then_inc(mlp_w_in, 16)
                if full < I:
                    sp.dma_start(raw[0:I - full, I // P, :], w[full:I]).then_inc(mlp_w_in, 16)

            if stop == 0:
                need(sp, x_add, B - 1, TB)
                sp.dma_start(out_v, x_sb[:, :, :]).then_inc(out_done, 16)
                sp.wait_ge(out_done, 16)
                sp.wait_ge(w12_in, 96)
                sp.wait_ge(mlp_w_in, 64)
                return
            if stop == 1:
                need(sp, ffn1.b2_add, T - 1, E)
                sp.dma_start(out_v, x_sb[:, :, :]).then_inc(out_done, 16)
                sp.wait_ge(out_done, 16)
                sp.wait_ge(mlp_w_in, 64)
                return

            need(sp, ffn1.pre, T - 1, 2)
            sp.dma_start(down_raw[:, :, :], w_down.rearrange("(c p) n -> p c n", p=P)).then_inc(down_in, 16)
            need(sp, mlp.turned, 3 * IC - 1, 1)
            for e in range(E):
                sp.dma_start(w1_sb[:, e], w1_in[e].rearrange("(c p) n -> p c n", p=P)).then_inc(w12_in2, 16)
            if stop == 2:
                need(sp, mlp.y_add, T - 1, 1)
                sp.dma_start(out_v, x_sb[:, :, :]).then_inc(out_done, 16)
                sp.wait_ge(out_done, 16)
                sp.wait_ge(w12_in2, 48)
                return
            for n in range(T):
                need(sp, ffn2.b2_add, n, E)
                sp.dma_start(out_v[:, n, :], x_sb[:, n, :]).then_inc(out_done, 16)
            sp.wait_ge(out_done, 16 * T)

        @block.gpsimd
        def _(pool):
            nc.gpsimd.memset(ident[:, :], 0.0).then_inc(ident_ok, 1)
            nc.gpsimd.memset(neg_half[:, :], -0.5).then_inc(ident_ok, 1)
            pool.wait_ge(ident_ok, 2)
            nc.gpsimd.affine_select(out=ident[:, :], in_=ident[:, :], compare_op=ALU.not_equal, fill=1.0,
                                    base=0, pattern=[[-1, P]], channel_multiplier=1).then_inc(ident_ok, 1)
            nc.gpsimd.memset(ones16[:, :], 1.0).then_inc(ident_ok, 1)

            def constants():
                nc.gpsimd.memset(maskS[:, :], 0.0).then_inc(consts, 1)
                nc.gpsimd.memset(maskT[:, :], 0.0).then_inc(consts, 1)
                nc.gpsimd.memset(vision[:, :], 1.0).then_inc(consts, 1)
                nc.gpsimd.memset(ones32[:, :], 1.0).then_inc(consts, 1)
                nc.gpsimd.memset(first_row[:, :], 1.0).then_inc(consts, 1)
                nc.gpsimd.memset(v_ones[:, :, :, HD:2 * HD], 1.0).then_inc(consts, 1)
                pool.wait_ge(ident_ok, 3)
                nc.gpsimd.tensor_copy(ident16[:, :], ident[:, :]).then_inc(consts, 1)
                pool.wait_ge(consts, 5)
                nc.gpsimd.affine_select(out=maskS[:, :], in_=maskS[:, :], compare_op=ALU.is_ge, fill=NEG,
                                        base=0, pattern=[[-1, P]], channel_multiplier=1).then_inc(consts, 1)
                nc.gpsimd.affine_select(out=maskT[:, :], in_=maskT[:, :], compare_op=ALU.is_ge, fill=NEG,
                                        base=0, pattern=[[1, P]], channel_multiplier=-1).then_inc(consts, 1)
                nc.gpsimd.affine_select(out=vision[:, :], in_=vision[:, :], compare_op=ALU.is_ge, fill=0.0,
                                        base=VISION - 1, pattern=[[0, P]], channel_multiplier=-1).then_inc(consts, 1)
                nc.gpsimd.affine_select(out=first_row[:, :], in_=first_row[:, :], compare_op=ALU.is_ge, fill=0.0,
                                        base=0, pattern=[[0, P]], channel_multiplier=-1).then_inc(consts, 1)
                pool.wait_ge(consts, 10)
                nc.gpsimd.tensor_tensor(text[:, :], ones32[:, :], vision[:, :], ALU.subtract).then_inc(consts, 1)
                for i in range(1 + 2 * 8):
                    nc.gpsimd.memset(numbers[:, i:i + 1], float(i)).then_inc(bits_set, 1)
                for i in range(BITS):
                    nc.gpsimd.memset(bits[:, i:i + 1], 1 << (BITS - 1 - i)).then_inc(bits_set, 1)

            def ln(b):
                need_apart(pool, stat, b, 2 * TB)
                nc.gpsimd.tensor_scalar(spread[:, :], moments[:, :, 1], EPS, None, ALU.add).then_inc(rstd_ok.sem, 1)
                need(pool, rstd_ok, b, 1)
                nc.gpsimd.tensor_tensor(rstd[:, :], spread[:, :], neg_half[:, :], ALU.pow).then_inc(rstd_ok.sem, 1)

            def cut(b):
                for f in range(4):
                    side, pair = f // 2, f % 2
                    need(pool, part2, b, f + 1)
                    r = resid[:, f % 2, :].rearrange("p (h t) -> p h t", h=2)
                    nc.gpsimd.tensor_tensor(parts[:, side, 2, 2 * pair:2 * pair + 2, :], r,
                                            parts[:, side, 1, 2 * pair:2 * pair + 2, :], ALU.subtract
                                            ).then_inc(part3.sem, 1)

            def values(b):
                need(pool, qv_out, b, 2 * TB)
                need_apart(pool, pv_ps, b - 1, NG)
                nc.gpsimd.tensor_copy(v_ones[:, :, :, 0:HD],
                                      v_stage[:, :, :].rearrange("p j (h d) -> p j h d", d=HD)).then_inc(v_copy.sem, 1)

            def norm(signals, step):
                need_apart(pool, signals.stat, step, 2)
                nc.gpsimd.tensor_scalar(ln_spread[:, :], ln_moments[:, 1:2], EPS, None,
                                        ALU.add).then_inc(signals.rstd.sem, 1)
                need(pool, signals.rstd, step, 1)
                nc.gpsimd.tensor_tensor(ln_rstd[:, :], ln_spread[:, :], neg_half[:, 0:1],
                                        ALU.pow).then_inc(signals.rstd.sem, 1)

            ln(0)
            constants()
            cut(0)
            values(0)
            ln(1)
            cut(1)
            values(1)
            with pool.Fori(0, B - 2) as b:
                ln(b + 2)
                cut(b + 2)
                for j in range(TB):
                    norm(norm2, tile_step(b, j, TB))
                values(b + 2)
            for b in (B - 2, B - 1):
                for j in range(TB):
                    norm(norm2, tile_step(b, j, TB))
            if stop == 0:
                return

            def take_row(ffn, n, i, before):
                need(pool, before.rows, n, 1)
                need_apart(pool, ffn.hT_ps, shift(n, -2), 1)
                nc.gpsimd.tensor_copy(h_cur[:, i, :], h_all[:, index(n), :]).then_inc(ffn.row.sem, 1)

            def ffn_pool(ffn, before, after):
                for n in range(2):
                    take_row(ffn, n, n, before)
                with pool.Fori(0, T // 2 - 1) as b:
                    for i in range(2):
                        take_row(ffn, Step(b, 2, 2 + i), i, before)
                        if after is not None:
                            norm(after, Step(b, 2, i))
                if after is not None:
                    for n in range(T - 2, T):
                        norm(after, n)

            ffn_pool(ffn1, norm2, norm3)
            if stop == 1:
                return
            for n in range(2):
                take_row(mlp, n, n, norm3)
            with pool.Fori(0, T // 2 - 1) as b:
                for i in range(2):
                    take_row(mlp, Step(b, 2, 2 + i), i, norm3)
                    norm(norm4, Step(b, 2, i))
            for n in range(T - 2, T):
                norm(norm4, n)
            if stop == 2:
                return
            ffn_pool(ffn2, norm4, None)

        @block.scalar
        def _(act):
            act.sem_inc(route1.mag.sem, 1)
            act.sem_inc(route2.mag.sem, 1)
            act.wait_ge(bias_zero, 1)
            for i in range(3):
                row = b_raw[32 * i:32 * i + 1]
                act.dma_start(row[:, B_ATTN:B_ATTN + 3 * D], b_attn.rearrange("(a n) -> a n", a=1)).then_inc(bias_in, 16)
            for i in range(3):
                row = b_raw[32 * i:32 * i + 1]
                act.dma_start(row[:, B_PROJ:B_PROJ + D], b_proj.rearrange("(a n) -> a n", a=1)).then_inc(bias_in2, 16)
                act.dma_start(row[:, B_1:B_1 + E * D], b1_in.rearrange("(a e) n -> a (e n)", a=1)).then_inc(bias_in2, 16)

            def project(b):
                for j in range(TB):
                    need(act, hT_ps, b, j + 1)
                    nc.scalar.copy(actT[:, :, j * P:(j + 1) * P],
                                   work[j].rearrange("p (c t) -> p c t", c=KC)).then_inc(hT_ok.sem, 1)
                for j in range(TB):
                    need(act, qkv_ps, b, 3 * j + 1)
                    nc.scalar.mul(qk_tok[:, j, 0:D], work[j % 2], SCALE).then_inc(qv_out.sem, 1)
                    need(act, qkv_ps, b, 3 * j + 3)
                    nc.scalar.copy(v_stage[:, j, :], work[j % 2]).then_inc(qv_out.sem, 1)

            def maxima(b):
                need(act, nmT_ps, b, 1)
                nc.scalar.copy(nmaxT[0:MAX_PARTS * H, :],
                               work[0].bitcast(BF16)[0:MAX_PARTS * H, 0:S]).then_inc(nmT_ok.sem, 1)
                need(act, nmT_ok, b, 1)
                for m in range(MAX_PARTS):
                    act.dma_start(qst[SROWS + m:SROWS + m + 1, :, :],
                                  nmaxT[m * H:(m + 1) * H, :]).then_inc(nm_in.sem, 16)

            def cut(b, fs):
                for f in fs:
                    side, pair = f // 2, f % 2
                    need(act, tr_ps, b, f + 1)
                    nc.scalar.copy(parts[:, side, 0, 2 * pair:2 * pair + 2, :],
                                   work[f % 2].rearrange("p (h t) -> p h t", h=2)).then_inc(part1.sem, 1)
                    if f >= 1:
                        second_part(b, f - 1)
                if 3 in fs:
                    second_part(b, 3)

            def second_part(b, f):
                side, pair = f // 2, f % 2
                need(act, res1, b, f + 1)
                nc.scalar.copy(parts[:, side, 1, 2 * pair:2 * pair + 2, :],
                               resid[:, f % 2, :].rearrange("p (h t) -> p h t", h=2)).then_inc(part2.sem, 1)

            def attend(b):
                for g in range(NG):
                    need(act, sT_ps, b, g + 1)
                    if g >= 2:
                        need(act, pv_ps, b, g - 1)
                    nc.scalar.activation(probsT[:, g % 2, :].rearrange("p (k n) -> p k n", k=3), slot[g % 2],
                                         ACT.Exp).then_inc(exp_ok.sem, 1)
                for j in range(TB):
                    need(act, oT_ps, b, j + 1)
                    nc.scalar.copy(actT[:, :, j * P:(j + 1) * P],
                                   work[j].rearrange("p (c t) -> p c t", c=KC)).then_inc(oT_ok.sem, 1)

            def magnitudes(norm, route, step):
                need(act, norm.rows, step, 1)
                t = index(step)
                need(act, route.mag, shift(step, -1), 1)
                nc.scalar.activation(abs_junk[:, :], h_all[:, t, :], ACT.Abs,
                                     accum_out=abs_sum[:, bass.ds(t, 1)]).then_inc(route.mag.sem, 1)

            project(0)
            cut(0, range(4))
            with act.Fori(0, B - 1) as b:
                project(b + 1)
                cut(b + 1, (0, 1))
                maxima(b)
                cut(b + 1, (2, 3))
                attend(b)
            maxima(B - 1)
            for t in range(T - 2 * TB):
                magnitudes(norm2, route1, t)
            attend(B - 1)
            for t in range(T - 2 * TB, T):
                magnitudes(norm2, route1, t)
            if stop == 0:
                return

            def route_act(route):
                need(act, route.shifted, 0, 1)
                nc.scalar.activation(tiny[:, 10, :], tiny[:, 0, :], ACT.Exp).then_inc(route.exp.sem, 1)

            def functions(ffn, n, i, s):
                need(act, ffn.pre, n, s + 1)
                need(act, ffn.mix, shift(n, -1), 4 * (s + 1))
                x = ps[:, 2 * i + s, :]
                nc.scalar.activation(funs[:, s, 0, :], x, ACT.Tanh).then_inc(ffn.fun.sem, 1)
                nc.scalar.activation(funs[:, s, 1, :], x, ACT.Gelu).then_inc(ffn.fun.sem, 1)
                nc.scalar.activation(funs[:, s, 2, :], x, ACT.Tanh, scale=0.5).then_inc(ffn.fun.sem, 1)

            def ffn_act_step(ffn, n, i, back, front, mid):
                if back:
                    for s in range(2):
                        need(act, ffn.aT_ps, shift(n, -2), s + 1)
                        nc.scalar.copy(aT[:, s, :, :], ps[:, 4 + s, :].rearrange("p (c t) -> p c t", c=KC)
                                       ).then_inc(ffn.aT.sem, 1)
                if front:
                    need(act, ffn.hT_ps, n, 1)
                    nc.scalar.copy(hT[:, i, :, :], ps[:, 7, :].rearrange("p (c t) -> p c t", c=KC)
                                   ).then_inc(ffn.hT.sem, 1)
                if mid:
                    functions(ffn, shift(n, -1), 1 - i, 1)
                if front:
                    functions(ffn, n, i, 0)

            def ffn_act(ffn):
                ffn_act_step(ffn, 0, 0, False, True, False)
                ffn_act_step(ffn, 1, 1, False, True, True)
                with act.Fori(0, T // 2 - 1) as b:
                    for i in range(2):
                        ffn_act_step(ffn, Step(b, 2, 2 + i), i, True, True, True)
                ffn_act_step(ffn, T, 0, True, False, True)
                ffn_act_step(ffn, T + 1, 1, True, False, False)

            route_act(route1)
            ffn_act(ffn1)
            if stop == 1:
                return

            def rows_of(u):
                return min(P, I - u % IC * P)

            for u in range(3 * IC):
                need(act, mlp.turned, u, 1)
                c, n = u % IC, rows_of(u)
                if u < 2 * IC:
                    nc.scalar.copy((wgT, wuT)[u // IC][:, :, c * P:c * P + n],
                                   ps[:, u % 6, :].rearrange("p (c t) -> p c t", c=KC)[:, :, 0:n]
                                   ).then_inc(mlp.kept.sem, 1)
                else:
                    nc.scalar.copy(wdT[0:n, c, :], ps[0:n, u % 6, :]).then_inc(mlp.kept.sem, 1)

            def gate_act(n, i):
                need(act, mlp.hT_ps, n, 1)
                nc.scalar.copy(hT[:, i, :, :], ps[:, ROW_BANK, :].rearrange("p (c t) -> p c t", c=KC)
                               ).then_inc(mlp.hT.sem, 1)

            def sizes(n):
                need(act, mlp.gate, n, 1)
                need(act, mlp.prod, shift(n, -1), 3)
                need(act, mlp.slow, shift(n, -1), SLOW)
                nc.scalar.activation(mlp_s[:, :], gate_ps, ACT.Silu).then_inc(mlp.silu.sem, 1)
                need(act, mlp.silu, n, 1)
                nc.scalar.activation(mlp_size[:, :], mlp_s[:, :], ACT.Abs,
                                     accum_out=size_sum[:, :]).then_inc(mlp.size.sem, 1)

            def mlp_act_step(n, i, back, front):
                if front:
                    gate_act(shift(n, 1), 1 - i)
                if front:
                    sizes(shift(n, 1))
                if back:
                    magnitudes(norm4, route2, shift(n, -1))

            gate_act(0, 0)
            sizes(0)
            mlp_act_step(0, 0, False, True)
            with act.Fori(0, T // 2 - 1) as b:
                for i in range(2):
                    mlp_act_step(Step(b, 2, 1 + i), 1 - i, True, True)
            mlp_act_step(T - 1, 1, True, False)
            magnitudes(norm4, route2, T - 1)
            if stop == 2:
                return
            route_act(route2)
            ffn_act(ffn2)

        @block.vector
        def _(dve):
            def ln(b, first):
                for j in range(TB):
                    x = x_sb[:, b * TB + j, :]
                    nc.vector.bn_stats(stats[:, j, :], x).then_inc(stat.sem, 1)
                need_apart(dve, stat, b, TB)
                for j in range(TB):
                    nc.vector.bn_aggr(moments[:, j, :], stats[:, j, :]).then_inc(stat.sem, 1)
                need(dve, rstd_ok, b, 2)
                for j in range(TB):
                    nc.vector.tensor_scalar(h_sb[:, j, :], x_sb[:, b * TB + j, :], moments[:, j, 0:1],
                                            rstd[:, j:j + 1], ALU.subtract, ALU.mult).then_inc(h_ok.sem, 1)

            def keys(b, j):
                need(dve, qkv_ps, b, 3 * j + 2)
                nc.vector.tensor_copy(qk_tok[:, j, D:2 * D], work[1 - j % 2]).then_inc(k_out.sem, 1)

            def residues(b):
                for f in range(4):
                    side, pair = f // 2, f % 2
                    need(dve, part1, b, f + 1)
                    if f >= 2:
                        need(dve, part3, b, f - 1)
                    r = resid[:, f % 2, :].rearrange("p (h t) -> p h t", h=2)
                    nc.vector.tensor_tensor(r, work[f % 2].rearrange("p (h t) -> p h t", h=2),
                                            parts[:, side, 0, 2 * pair:2 * pair + 2, :],
                                            ALU.subtract).then_inc(res1.sem, 1)

            def maxima(b, between):
                for g in range(NG):
                    need(dve, s_ps, b, g + 1)
                    sl = slot[g % 2]
                    nc.vector.tensor_reduce(nmax[:, 0, g * G:(g + 1) * G],
                                            sl[:, 0, :].rearrange("p (h k) -> p h k", h=G),
                                            AX.X, ALU.max, negate=True).then_inc(max_ok.sem, 1)
                    nc.vector.tensor_reduce(nmax[:, 1, g * G:(g + 1) * G],
                                            sl[:, 1:3, :].rearrange("p s (h k) -> p (s h) k", h=2),
                                            AX.X, ALU.max, negate=True).then_inc(max_ok.sem, 1)
                    between(g)
                need(dve, max_ok, b, 2 * NG)
                nc.vector.tensor_copy(nmax_p[:, :, 0, :], nmax[:, :, :]).then_inc(nm_cut.sem, 1)
                need(dve, nm_cut, b, 1)
                nc.vector.tensor_tensor(nmax_r[:, :, :], nmax[:, :, :], nmax_p[:, :, 0, :],
                                        ALU.subtract).then_inc(nm_cut.sem, 1)
                need(dve, nm_cut, b, 2)
                nc.vector.tensor_copy(nmax_p[:, :, 1, :], nmax_r[:, :, :]).then_inc(nm_cut.sem, 1)
                need(dve, nm_cut, b, 3)
                nc.vector.tensor_tensor(nmax_p[:, :, 2, :], nmax_r[:, :, :], nmax_p[:, :, 1, :],
                                        ALU.subtract).then_inc(nm_cut.sem, 1)

            def second_norm(b, j, part):
                t = tile_step(b, j, TB)
                if part == 0:
                    norm_stats(norm2, t)
                elif part == 1:
                    norm_rows(norm2, t)
                else:
                    logit_rows(norm2, route1, t)

            def attend(b, tail):
                def normalise(g):
                    need(dve, oTr_ps, b, g + 1)
                    o = work[g % 2][:, S:2 * S].rearrange("p (j h e) -> p j h e", j=TB, h=G)
                    nc.vector.reciprocal(rden[:, g % 2, :].rearrange("p (j h) -> p j h", j=TB),
                                         o[:, :, :, HD]).then_inc(rden_ok.sem, 1)
                    need(dve, rden_ok, b, g + 1)
                    r = rden[:, g % 2, :].rearrange("p (j h) -> p j h", j=TB).unsqueeze(3)
                    nc.vector.tensor_tensor(
                        o_tok[:, :, g * G * HD:(g + 1) * G * HD].rearrange("p j (h d) -> p j h d", h=G),
                        o[:, :, :, 0:HD], r.broadcast_to([P, TB, G, HD]), ALU.mult).then_inc(norm_ok.sem, 1)

                for g in range(NG):
                    need(dve, pv_ps, b, g + 1)
                    nc.vector.tensor_copy(outT[:, g % 2, :], work[g % 2][:, 0:S]).then_inc(outT_ok.sem, 1)
                    if g >= 1:
                        normalise(g - 1)
                    if tail and g < 2 * 3:
                        second_norm(b - 1, g // 3, g % 3)
                normalise(NG - 1)
                for j in range(TB):
                    need(dve, y_ps, b, j + 1)
                    x = x_sb[:, b * TB + j, :]
                    nc.vector.tensor_tensor(x, work[j], x, ALU.add).then_inc(x_add.sem, 1)

            def norm(signals, step):
                norm_stats(signals, step)
                norm_rows(signals, step)

            def norm_stats(signals, step):
                x = x_sb[:, index(step), :]
                nc.vector.bn_stats(ln_stats[:, :], x).then_inc(signals.stat.sem, 1)
                need_apart(dve, signals.stat, step, 1)
                nc.vector.bn_aggr(ln_moments[:, :], ln_stats[:, :]).then_inc(signals.stat.sem, 1)

            def norm_rows(signals, step):
                x = x_sb[:, index(step), :]
                need(dve, signals.rstd, step, 2)
                nc.vector.tensor_scalar(h_all[:, index(step), :], x, ln_moments[:, 0:1], ln_rstd[:, :],
                                        ALU.subtract, ALU.mult).then_inc(signals.rows.sem, 1)

            def logit_rows(norm, route, step):
                need(dve, norm.rows, step, 1)
                t = index(step)
                for e in range(E):
                    need(dve, route.logit, step, e)
                    nc.vector.scalar_tensor_tensor(out=junk[:, :], in0=h_all[:, t, :], scalar=1.0,
                                                   in1=gate_v[:, 0:D, e], op0=ALU.mult, op1=ALU.mult,
                                                   accum_out=logits[:, t, e:e + 1]).then_inc(route.logit.sem, 1)

            def cut_bias(lo, hi, n):
                r = t = b_raw[0:65, lo:hi]
                nc.vector.tensor_copy(b_p1[0:65, lo:hi], r).then_inc(bias_cut, 1)
                dve.wait_ge(bias_cut, n + 1)
                nc.vector.tensor_tensor(t, r, b_p1[0:65, lo:hi], ALU.subtract).then_inc(bias_cut, 1)
                dve.wait_ge(bias_cut, n + 2)
                nc.vector.tensor_copy(b_p2[0:65, lo:hi], t).then_inc(bias_cut, 1)
                nc.vector.tensor_copy(bias3[0:1, lo:hi], b_p1[0:1, lo:hi]).then_inc(bias_cut, 1)
                dve.wait_ge(bias_cut, n + 3)
                nc.vector.tensor_copy(bias3[32:33, lo:hi], b_p2[32:33, lo:hi]).then_inc(bias_cut, 1)
                nc.vector.tensor_tensor(bias3[64:65, lo:hi], t[64:65], b_p2[64:65, lo:hi],
                                        ALU.subtract).then_inc(bias_cut, 1)

            nc.vector.memset(b_raw[0:65, :], 0.0).then_inc(bias_zero, 1)
            nc.vector.memset(bias3[0:65, :], 0.0).then_inc(bias_zero, 1)
            dve.sem_inc(x_add.sem, TB)
            dve.sem_inc(route1.logit.sem, 1)
            dve.sem_inc(route2.logit.sem, 1)
            dve.wait_ge(x_first, 16)
            ln(0, True)
            dve.wait_ge(bias_in, 48)
            dve.wait_ge(bias_zero, 2)
            cut_bias(B_ATTN, B_ATTN + 3 * D, 0)
            for j in range(TB):
                keys(0, j)
            residues(0)
            dve.wait_ge(bias_in2, 96)
            cut_bias(B_PROJ, NBIAS, 6)
            dve.wait_ge(x_rest, 16)
            dve.wait_ge(gate_in, 48)
            def step(b, tail):
                ln(b + 1, True)
                maxima(b, lambda g: keys(b + 1, (g - 2) // 3) if g in (2, 5) else None)
                residues(b + 1)
                attend(b, tail)

            step(0, False)
            with dve.Fori(0, B - 2) as b:
                step(b + 1, True)
            maxima(B - 1, lambda g: None)
            attend(B - 1, True)
            for j in range(TB):
                dve.wait_ge(x_add.sem, x_add.count(B - 1, TB))
                for part in range(3):
                    second_norm(B - 1, j, part)
            if stop == 0:
                return

            def route_dve(route):
                done = [0]

                def link(ins):
                    done[0] += 1
                    ins.then_inc(route.chain.sem, 1)
                    dve.wait_ge(route.chain.sem, done[0])

                def row(i, n):
                    return tiny[:, i, 0:n]

                tt, ts = nc.vector.tensor_tensor, nc.vector.tensor_scalar
                need(dve, route.logit, T - 1, E)
                need(dve, route.sums, 0, 1)
                ratio, vis = row(3, B), row(4, B)
                link(ts(vis, ps[:, 6, 0:B], 1.0 / (VISION * D), 1e-8, ALU.mult, ALU.add))
                link(nc.vector.reciprocal(row(5, B), vis))
                link(nc.vector.scalar_tensor_tensor(out=ratio, in0=ps[:, 6, B:2 * B], scalar=1.0 / ((S - VISION) * D),
                                                    in1=row(5, B), op0=ALU.mult, op1=ALU.mult))
                rg = row(6, B * E).rearrange("p (b e) -> p b e", b=B)
                link(tt(rg, ratio.unsqueeze(2).broadcast_to([P, B, E]),
                        gate_v[:, D:D + 1, :].broadcast_to([P, B, E]), ALU.mult))
                link(tt(rg, rg, gate_bias[:, :].unsqueeze(1).broadcast_to([P, B, E]), ALU.add))
                lg = row(7, T * E).rearrange("p (t e) -> p t e", t=T)
                link(tt(lg.rearrange("p (b j) e -> p b j e", b=B), logits[:, :, :].rearrange("p (b j) e -> p b j e", b=B),
                        rg.unsqueeze(2).broadcast_to([P, B, TB, E]), ALU.add))
                link(nc.vector.tensor_reduce(row(8, T), lg, AX.X, ALU.max))
                tt(row(0, T * E).rearrange("p (t e) -> p t e", t=T), lg,
                   row(8, T).unsqueeze(2).broadcast_to([P, T, E]), ALU.subtract).then_inc(route.shifted.sem, 1)
                need(dve, route.exp, 0, 1)
                ex = row(10, T * E).rearrange("p (t e) -> p t e", t=T)
                link(nc.vector.tensor_reduce(row(8, T), ex, AX.X, ALU.add))
                link(nc.vector.reciprocal(row(11, T), row(8, T)))
                p = row(12, T * E).rearrange("p (t e) -> p t e", t=T)
                link(tt(p, ex, row(11, T).unsqueeze(2).broadcast_to([P, T, E]), ALU.mult))
                pf = p.rearrange("p (b j) e -> p b j e", b=B)[:, :, 0, :]
                ab, ac, bc = row(14, B), row(15, B), row(16, B)
                link(tt(ab, pf[:, :, 0], pf[:, :, 1], ALU.is_ge))
                link(tt(ac, pf[:, :, 0], pf[:, :, 2], ALU.is_ge))
                link(tt(bc, pf[:, :, 1], pf[:, :, 2], ALU.is_ge))
                rank = row(17, E * B).rearrange("p (e b) -> p e b", e=E)
                link(tt(rank[:, 0, :], ab, ac, ALU.add))
                link(ts(rank[:, 0, :], rank[:, 0, :], -1.0, 2.0, ALU.mult, ALU.add))
                link(tt(rank[:, 1, :], ab, bc, ALU.subtract))
                link(ts(rank[:, 1, :], rank[:, 1, :], 1.0, None, ALU.add))
                link(tt(rank[:, 2, :], ac, bc, ALU.add))
                sel = row(19, 2 * E * B)
                for s_ in range(2):
                    link(ts(sel[:, s_ * E * B:(s_ + 1) * E * B], row(17, E * B), float(s_), None, ALU.is_equal))
                sv = sel.rearrange("p (s e b) -> p s e b", s=2, e=E)
                link(nc.vector.scalar_tensor_tensor(out=experts[:, :, :], in0=sv[:, :, 2, :], scalar=2.0,
                                                    in1=sv[:, :, 1, :], op0=ALU.mult, op1=ALU.add))
                nc.vector.tensor_copy(row(20, T * E).bitcast(BF16)[:, 0:2 * E * B], sel).then_inc(route.rank.sem, 1)
                a, b, c = p[:, :, 0], p[:, :, 1], p[:, :, 2]
                top = row(13, 2 * T).rearrange("p (s t) -> p s t", s=2)
                link(tt(row(14, T), a, b, ALU.max))
                link(tt(row(15, T), a, b, ALU.min))
                link(tt(top[:, 0, :], row(14, T), c, ALU.max))
                link(tt(row(16, T), row(14, T), c, ALU.min))
                link(tt(top[:, 1, :], row(15, T), row(16, T), ALU.max))
                link(tt(row(17, T), top[:, 0, :], top[:, 1, :], ALU.add))
                link(ts(row(17, T), row(17, T), 1e-8, None, ALU.add))
                link(nc.vector.reciprocal(row(18, T), row(17, T)))
                link(tt(top, top, row(18, T).unsqueeze(1).broadcast_to([P, 2, T]), ALU.mult))
                need(dve, route.spread, 0, 1)
                link(nc.vector.tensor_copy(sel, ps[:, 6, 0:2 * E * B]))
                for s_ in range(2):
                    for e in range(E):
                        link(tt(coef[:, s_, :, e].rearrange("p (b j) -> p b j", b=B),
                                top[:, s_, :].rearrange("p (b j) -> p b j", b=B),
                                sv[:, s_, e, :].unsqueeze(2).broadcast_to([P, B, TB]), ALU.mult))
                link(tt(coef_b2[:, :, :], coef[:, 0, :, :], coef[:, 1, :, :], ALU.add))
                ts(coef[:, :, :, 2], coef[:, :, :, 2], 0.5, None, ALU.mult).then_inc(route.coef.sem, 1)
                need(dve, route.coef, 0, 1)

            def mix(ffn, n, i, s):
                t = index(n)
                x = ps[:, 2 * i + s, :]
                c = [coef[:, s, t, e:e + 1] for e in range(E)]
                u = funs[:, s, 2, :]
                k = 4 * s
                need(dve, ffn.fun, n, 3 * s + 3)
                nc.vector.tensor_scalar(u, u, c[2], c[2], ALU.mult, ALU.add).then_inc(ffn.mix.sem, 1)
                need(dve, ffn.mix, n, k + 1)
                nc.vector.tensor_tensor(u, x, u, ALU.mult).then_inc(ffn.mix.sem, 1)
                need(dve, ffn.mix, n, k + 2)
                nc.vector.scalar_tensor_tensor(out=u, in0=funs[:, s, 1, :], scalar=c[1], in1=u,
                                               op0=ALU.mult, op1=ALU.add).then_inc(ffn.mix.sem, 1)
                need(dve, ffn.mix, n, k + 3)
                nc.vector.scalar_tensor_tensor(out=act_tok[:, i, s, :], in0=funs[:, s, 0, :], scalar=c[0], in1=u,
                                               op0=ALU.mult, op1=ALU.add).then_inc(ffn.mix.sem, 1)

            def finish(ffn, n, after, route):
                need(dve, ffn.y_ps, n, 1)
                t = index(n)
                x = x_sb[:, t, :]
                nc.vector.tensor_tensor(x, ps[:, 6, :], x, ALU.add).then_inc(ffn.y_add.sem, 1)
                need(dve, ffn.y_add, n, 1)
                for e in range(E):
                    nc.vector.scalar_tensor_tensor(out=x, in0=b2_row[:, e, :], scalar=coef_b2[:, t, e:e + 1], in1=x,
                                                   op0=ALU.mult, op1=ALU.add).then_inc(ffn.b2_add.sem, 1)
                    need_apart(dve, ffn.b2_add, n, e + 1)
                if after is not None:
                    norm(after, n)

            def ffn_dve_step(ffn, n, i, after, back, front, mid):
                if mid:
                    mix(ffn, shift(n, -1), 1 - i, 1)
                if back:
                    finish(ffn, shift(n, -2), after, None)
                if front:
                    mix(ffn, n, i, 0)

            def ffn_dve(ffn, after):
                dve.sem_inc(ffn.y_add.sem, 1)
                ffn_dve_step(ffn, 0, 0, after, False, True, False)
                ffn_dve_step(ffn, 1, 1, after, False, True, True)
                with dve.Fori(0, T // 2 - 1) as b:
                    for i in range(2):
                        ffn_dve_step(ffn, Step(b, 2, 2 + i), i, after, True, True, True)
                ffn_dve_step(ffn, T, 0, after, True, False, True)
                ffn_dve_step(ffn, T + 1, 1, after, True, False, False)

            route_dve(route1)
            ffn_dve(ffn1, norm3)
            if stop == 1:
                return

            def search(n):
                k = [0]

                def link(ins):
                    ins.then_inc(mlp.pick.sem, 1)
                    k[0] += 1
                    need(dve, mlp.pick, n, k[0])

                need_apart(dve, mlp.size, n, 1)
                link(nc.vector.tensor_scalar(guess[:, :], size_sum[:, :], FIRST_GUESS / I, None, ALU.mult))
                for probe in range(PROBES - 1):
                    link(nc.vector.tensor_scalar(mlp_flag[:, :], mlp_size[:, :], guess[:, :], None, ALU.is_ge, ALU.add,
                                                 accum_out=cut_count[:, :]))
                    link(nc.vector.tensor_scalar(guess_step[:, :], cut_count[:, :], STEP, 1.0 - STEP * AIM,
                                                 ALU.mult, ALU.add))
                    link(nc.vector.tensor_tensor(guess[:, :], guess[:, :], guess_step[:, :], ALU.mult))
                link(nc.vector.tensor_scalar(mlp_flag[:, :], mlp_size[:, :], guess[:, :], None, ALU.is_ge, ALU.add,
                                             accum_out=cut_count[:, :]))
                link(nc.vector.tensor_scalar(short[:, :], cut_count[:, :], -1.0, float(KEEP), ALU.mult, ALU.add))
                link(nc.vector.tensor_copy(ladder[:, 0:1], guess[:, :]))
                need_apart(dve, mlp.prodT_ps, shift(n, -1), 3)
                link(nc.vector.scalar_tensor_tensor(out=mlp_prod[:, :], in0=mlp_size[:, :], scalar=guess[:, :],
                                                    in1=mlp_size[:, :], op0=ALU.is_lt, op1=ALU.mult))
                need_apart(dve, mlp.pick, n, k[0])
                link(nc.vector.max(ladder[:, 1:9], mlp_prod[:, :]))
                link(nc.vector.scalar_tensor_tensor(out=mlp_prod[:, :], in0=mlp_prod[:, :], scalar=ladder[:, 8:9],
                                                    in1=mlp_prod[:, :], op0=ALU.is_lt, op1=ALU.mult))
                need_apart(dve, mlp.pick, n, k[0])
                link(nc.vector.max(ladder[:, 9:17], mlp_prod[:, :]))
                link(nc.vector.scalar_tensor_tensor(out=pickout[:, :], in0=numbers[:, :], scalar=short[:, :],
                                                    in1=ladder[:, :], op0=ALU.is_equal, op1=ALU.mult,
                                                    accum_out=threshold[:, :]))
                link(nc.vector.tensor_scalar(mlp_flag[:, :], mlp_size[:, :], threshold[:, :], None, ALU.is_ge, ALU.add,
                                             accum_out=cut_count[:, :]))
                link(nc.vector.tensor_scalar(failed[:, :], cut_count[:, :], float(KEEP), None, ALU.not_equal))
                assert k[0] == PICKS, (k[0], PICKS)

            def product(n):
                need(dve, mlp.up, n, 1)
                nc.vector.tensor_tensor(mlp_prod[:, :], mlp_s[:, :], up_ps, ALU.mult).then_inc(mlp.prod.sem, 1)
                need(dve, mlp.prod, n, 1)
                nc.vector.tensor_tensor(mlp_prod[:, :], mlp_prod[:, :], mlp_flag[:, :], ALU.mult
                                        ).then_inc(mlp.prod.sem, 1)
                need_apart(dve, mlp.check, n, 1)
                nc.vector.tensor_copy(failures[0:1, :], check_ps).then_inc(mlp.prod.sem, 1)
                need_apart(dve, mlp.prod, n, 3)
                some = dve.value_load(failures[0:1, 0:1], min_val=0, max_val=P)
                with dve.If(some > 0):
                    search_bits(n)
                with dve.Else():
                    dve.sem_inc(mlp.slow.sem, SLOW)

            def search_bits(n):
                nc.vector.memset(cut_at[:, :], 0).then_inc(mlp.slow.sem, 1)
                with dve.Fori(0, BITS) as bit:
                    def after(k):
                        dve.wait_ge(mlp.slow.sem, mlp.slow.count(n, 1) + (bit * 4 + k))

                    after(0)
                    nc.vector.tensor_tensor(cut_try[:, :], cut_at[:, :], bits[:, bass.ds(bit, 1)],
                                            ALU.bitwise_or).then_inc(mlp.slow.sem, 1)
                    after(1)
                    nc.vector.tensor_scalar(mlp_flag[:, :], mlp_size[:, :], cut_try[:, :].bitcast(F32), None,
                                            ALU.is_ge, ALU.add, accum_out=cut_count[:, :]).then_inc(mlp.slow.sem, 1)
                    after(2)
                    nc.vector.scalar_tensor_tensor(out=cut_add[:, :], in0=cut_count[:, :], scalar=float(KEEP),
                                                   in1=bits[:, bass.ds(bit, 1)], op0=ALU.is_ge,
                                                   op1=ALU.mult).then_inc(mlp.slow.sem, 1)
                    after(3)
                    nc.vector.tensor_tensor(cut_at[:, :], cut_at[:, :], cut_add[:, :],
                                            ALU.bitwise_or).then_inc(mlp.slow.sem, 1)
                k = [1 + 4 * BITS]

                def link(ins):
                    ins.then_inc(mlp.slow.sem, 1)
                    k[0] += 1
                    if k[0] < SLOW:
                        need(dve, mlp.slow, n, k[0])

                need(dve, mlp.slow, n, k[0])
                cut = cut_at[:, :].bitcast(F32)
                link(nc.vector.tensor_scalar(mlp_flag[:, :], mlp_size[:, :], cut, None,
                                             ALU.is_ge, ALU.add, accum_out=cut_count[:, :]))
                link(nc.vector.tensor_scalar(surplus[:, :], cut_count[:, :], -float(KEEP), None, ALU.add))
                link(nc.vector.tensor_scalar(mlp_flag[:, :], mlp_size[:, :], cut, None, ALU.is_equal))
                link(nc.vector.tensor_tensor_scan(mlp_prod[:, :], mlp_flag[:, :], mlp_flag[:, :], 0.0,
                                                  ALU.add, ALU.bypass))
                link(nc.vector.scalar_tensor_tensor(out=mlp_flag[:, :], in0=mlp_prod[:, :], scalar=surplus[:, :],
                                                    in1=mlp_flag[:, :], op0=ALU.is_le, op1=ALU.mult))
                link(nc.vector.scalar_tensor_tensor(out=mlp_flag[:, :], in0=mlp_size[:, :], scalar=cut,
                                                    in1=mlp_flag[:, :], op0=ALU.is_ge, op1=ALU.subtract))
                link(nc.vector.tensor_tensor(mlp_prod[:, :], mlp_s[:, :], up_ps, ALU.mult))
                link(nc.vector.tensor_tensor(mlp_prod[:, :], mlp_prod[:, :], mlp_flag[:, :], ALU.mult))
                assert k[0] == SLOW

            def mlp_finish(n, i):
                need(dve, mlp.y_ps, n, 1)
                x = x_sb[:, index(n), :]
                nc.vector.tensor_tensor(x, ps[:, Y_BANK, :], x, ALU.add).then_inc(mlp.y_add.sem, 1)
                need_apart(dve, mlp.y_add, n, 1)
                norm(norm4, n)
                logit_rows(norm4, route2, n)

            dve.sem_inc(mlp.y_add.sem, 1)
            dve.wait_ge(bits_set, BITS + 17)

            def mlp_dve_step(n, i, back):
                search(n)
                if back:
                    mlp_finish(shift(n, -1), 1 - i)
                product(n)
                keep_product(n)

            def keep_product(n):
                for k in range(3):
                    need(dve, mlp.prodT_ps, n, k + 1)
                    chunks = min(4, IC - 4 * k)
                    if k == 2 and I % P:
                        chunks -= 1
                    nc.vector.tensor_copy(prodT[:, 4 * k:4 * k + chunks, :],
                                   ps[:, PROD_BANK[k], 0:chunks * P].rearrange("p (c t) -> p c t", t=P)
                                   ).then_inc(mlp.prodT.sem, 1)
                    if k == 2:
                        m = I - I // P * P
                        nc.vector.tensor_copy(prodT[0:m, IC - 1, :], ps[0:m, PROD_BANK[2], chunks * P:(chunks + 1) * P]
                                       ).then_inc(mlp.prodT.sem, 1)

            mlp_dve_step(0, 0, False)
            with dve.Fori(0, T // 2 - 1) as b:
                for i in range(2):
                    mlp_dve_step(Step(b, 2, 1 + i), 1 - i, True)
            mlp_dve_step(T - 1, 1, True)
            mlp_finish(T - 1, 1)
            if stop == 2:
                return
            route_dve(route2)
            ffn_dve(ffn2, None)

        @block.tensor
        def _(pe):
            def biased(out_ap, at_col, first):
                return nc.tensor.matmul(out_ap, ones16[0:65, :], bias3[0:65, at_col:at_col + D], start=first, stop=False)

            def turn_rows(b):
                need(pe, h_ok, b, TB)
                for j in range(TB):
                    need(pe, x_add, b - 2, j + 1)
                    for c in range(KC):
                        m = nc.tensor.transpose(work[j][:, c * P:(c + 1) * P],
                                                h_sb[:, j, c * P:(c + 1) * P], ident[:, :])
                    m.then_inc(hT_ps.sem, 1)

            def project_part(b, j, n, wait_bias=None):
                w = work[(3 * j + n) % 2]
                if j == 0 and n == 0:
                    need(pe, hT_ok, b, 1)
                elif j == 0 and n == 1:
                    need(pe, hT_ok, b, 2)
                elif (j, n) in ((0, 2), (1, 1), (1, 2)):
                    need(pe, qv_out, b, {(0, 2): 1, (1, 1): 2, (1, 2): 3}[(j, n)])
                else:
                    need(pe, k_out, b, 1)
                for c in range(KC):
                    nc.tensor.matmul(w, actT[:, c, j * P:(j + 1) * P], wqkv[:, c, n * D:(n + 1) * D],
                                     start=(c == 0), stop=False)
                if wait_bias:
                    wait_bias()
                nc.tensor.matmul(w, ones16[0:65, :], bias3[0:65, B_ATTN + n * D:B_ATTN + (n + 1) * D],
                                 start=False, stop=True).then_inc(qkv_ps.sem, 1)

            def project(b, wait_bias):
                for j in range(TB):
                    for n in range(3):
                        project_part(b, j, n, wait_bias if (j, n) == (0, 0) else None)

            def turn(b, before, fs):
                for f in fs:
                    side, pair = f // 2, f % 2
                    if f == 0:
                        need(pe, qv_out, b, 3)
                        need(pe, k_out, b, 2)
                    elif f == 1:
                        need(pe, qv_out, b, 4)
                    elif f == 2:
                        need(pe, res1, b, 1)
                        need(pe, nmT_ok, before, 1)
                    else:
                        need(pe, res1, b, f - 1)
                    for i in range(2):
                        for j in range(TB):
                            m = nc.tensor.transpose(
                                work[f % 2][:, i * S + j * P:i * S + (j + 1) * P],
                                qk_tok[:, j, side * D + (2 * pair + i) * P:side * D + (2 * pair + i + 1) * P],
                                ident[:, :])
                    m.then_inc(tr_ps.sem, 1)

            def masked(bank, mask, cols):
                return nc.tensor.matmul(cols, ident16[:, :], mask, start=True, stop=False, skip_group_check=True)

            def diagonal(mask, n):
                return mask[:, :].unsqueeze(1).broadcast_to([P, n, P])

            def scores(b, between):
                for g in range(NG):
                    if g % GHALF == 0:
                        need(pe, scat[g // GHALF], b, scat[g // GHALF].per)
                    sl = slot[g % 2]
                    if g >= 2:
                        need(pe, max_ok, b, 2 * (g - 1))
                    nc.tensor.matmul(sl[:, 0, :].rearrange("p (h k) -> p h k", h=G), ident16[:, :], diagonal(maskS, G),
                                     start=True, stop=False, skip_group_check=True)
                    for s in range(2):
                        nc.tensor.matmul(sl[:, 1 + s, :].rearrange("p (h k) -> p h k", h=2)[:, :, P:S], ident16[:, :],
                                         diagonal(maskS, 2), start=True, stop=False, skip_group_check=True)
                    for i in range(G):
                        h = g * G + i
                        nc.tensor.matmul(sl[:, 0, i * P:(i + 1) * P], qst[0:SROWS, h, 0:P],
                                         kst[0:SROWS, h, 0:P], start=False, stop=True, skip_group_check=True)
                        m = nc.tensor.matmul(sl[:, 1 + i // 2, (i % 2) * S:(i % 2 + 1) * S],
                                             qst[0:SROWS, h, P:S], kst[0:SROWS, h, :],
                                             start=False, stop=True, skip_group_check=True)
                    m.then_inc(s_ps.sem, 1)
                    between(g)

            def maxima(b, wait_bank):
                need(pe, nm_cut, b, 4)
                wait_bank()
                for j in range(TB):
                    m = nc.tensor.transpose(work[0].bitcast(BF16)[0:MAX_PARTS * H, j * P:(j + 1) * P],
                                            nmax_p[:, j, :, :].rearrange("p m h -> p (m h)"), ident16[:, :])
                m.then_inc(nmT_ps.sem, 1)

            def scores_t(b, g):
                sl = slot[g % 2]
                if g >= 2:
                    need(pe, exp_ok, b, g - 1)
                nc.tensor.matmul(sl[:, 0, :].rearrange("p (h k) -> p h k", h=G), ident16[:, :], diagonal(maskT, G),
                                 start=True, stop=False, skip_group_check=True)
                for s in range(2):
                    nc.tensor.matmul(sl[:, 1 + s, :].rearrange("p (h k) -> p h k", h=2)[:, :, 0:P], ident16[:, :],
                                     diagonal(maskT, 2), start=True, stop=False, skip_group_check=True)
                for i in range(G):
                    h = g * G + i
                    nc.tensor.matmul(sl[:, 0, i * P:(i + 1) * P], kst[0:MROWS, h, P:S],
                                     qst[0:MROWS, h, P:S], start=False, stop=True, skip_group_check=True)
                    m = nc.tensor.matmul(sl[:, 1 + i // 2, (i % 2) * S:(i % 2 + 1) * S],
                                         kst[0:MROWS, h, 0:P], qst[0:MROWS, h, :],
                                         start=False, stop=True, skip_group_check=True)
                m.then_inc(sT_ps.sem, 1)

            def weigh(b, g):
                need(pe, exp_ok, b, g + 1)
                w = work[g % 2]
                for i in range(G):
                    h = g * G + i
                    nc.tensor.matmul(w[32 * i:32 * i + 2 * HD, 0:S], v_ones[:, 0, h, :],
                                     probsT[:, g % 2, D + i * S:D + (i + 1) * S],
                                     start=True, stop=False, tile_position=(0, 32 * i), skip_group_check=True)
                for i in range(G):
                    h = g * G + i
                    m = nc.tensor.matmul(w[32 * i:32 * i + 2 * HD, P:S], v_ones[:, 1, h, :],
                                         probsT[:, g % 2, i * P:(i + 1) * P],
                                         start=False, stop=True, tile_position=(0, 32 * i), skip_group_check=True)
                m.then_inc(pv_ps.sem, 1)

            def back(b, g):
                need(pe, outT_ok, b, g + 1)
                for j in range(TB):
                    m = nc.tensor.transpose(work[g % 2][:, S + j * P:S + (j + 1) * P],
                                            outT[:, g % 2, j * P:(j + 1) * P], ident[:, :])
                m.then_inc(oTr_ps.sem, 1)

            def attend(b, last):
                need(pe, nm_in, b, nm_in.per)
                need(pe, v_copy, b, 1)
                for g in range(NG + 2):
                    if g < NG:
                        scores_t(b, g)
                    if 1 <= g <= NG:
                        n = g - 1
                        if n >= 2:
                            need(pe, norm_ok, b, n - 1)
                        elif last:
                            need(pe, x_add, b - 1, TB)
                        else:
                            need(pe, res1, b + 1, 4)
                        weigh(b, n)
                    if g >= 2:
                        back(b, g - 2)
                need(pe, norm_ok, b, NG)
                for j in range(TB):
                    for c in range(KC):
                        m = nc.tensor.transpose(work[j][:, c * P:(c + 1) * P], o_tok[:, j, c * P:(c + 1) * P],
                                                ident[:, :])
                    m.then_inc(oT_ps.sem, 1)
                for j in range(TB):
                    need(pe, oT_ok, b, j + 1)
                    for c in range(KC):
                        nc.tensor.matmul(work[j], actT[:, c, j * P:(j + 1) * P], wproj[:, c, :],
                                         start=(c == 0), stop=False)
                    nc.tensor.matmul(work[j], ones16[0:65, :], bias3[0:65, B_PROJ:B_PROJ + D],
                                     start=False, stop=True).then_inc(y_ps.sem, 1)

            pe.wait_ge(ident_ok, 4)
            turn_rows(0)
            pe.wait_ge(wqkv_in, 16 * KC)
            project(0, lambda: pe.wait_ge(bias_cut, 6))
            pe.wait_ge(consts, 11)
            turn(0, -1, range(4))
            pe.wait_ge(alibi_in, 32)
            pe.wait_ge(wproj_in, 16)
            pe.wait_ge(bias_cut, 12)
            with pe.Fori(0, B - 1) as b:
                def between(g):
                    if g == 0:
                        turn_rows(b + 1)
                    elif g <= 3 * TB:
                        project_part(b + 1, (g - 1) // 3, (g - 1) % 3)

                scores(b, between)
                turn(b + 1, b, (0, 1))
                maxima(b, lambda: need(pe, res1, b + 1, 1))
                turn(b + 1, b, (2, 3))
                attend(b, False)
            scores(B - 1, lambda g: None)
            maxima(B - 1, lambda: need(pe, x_add, B - 2, 1))
            attend(B - 1, True)
            if stop == 0:
                return

            def route_pe(route):
                need(pe, route.mag, T - 1, 1)
                first, second = abs_sum[:, 0:T:2], abs_sum[:, 1:T:2]
                nc.tensor.matmul(ps[:, 6, 0:B], vision[:, :], first, start=True, stop=True, skip_group_check=True)
                nc.tensor.matmul(ps[:, 6, B:2 * B], text[:, :], first, start=True, stop=False, skip_group_check=True)
                nc.tensor.matmul(ps[:, 6, B:2 * B], ones32[:, :], second, start=False, stop=True,
                                 skip_group_check=True).then_inc(route.sums.sem, 1)
                need(pe, route.rank, 0, 1)
                nc.tensor.matmul(ps[:, 6, 0:2 * E * B], first_row[:, :], tiny[:, 20, :].bitcast(BF16)[:, 0:2 * E * B],
                                 start=True, stop=True).then_inc(route.spread.sem, 1)

            def ffn_pe_step(ffn, n, i, back, front):
                m = shift(n, -2)
                if back:
                    for s in range(2):
                        need(pe, ffn.mix, m, 4 * s + 4)
                        for c in range(KC):
                            last = nc.tensor.transpose(ps[:, 4 + s, c * P:(c + 1) * P],
                                                       act_tok[:, i, s, c * P:(c + 1) * P], ident[:, :])
                        last.then_inc(ffn.aT_ps.sem, 1)
                if front:
                    need(pe, ffn.row, n, 1)
                    for c in range(KC):
                        last = nc.tensor.transpose(ps[:, 7, c * P:(c + 1) * P], h_cur[:, i, c * P:(c + 1) * P],
                                                   ident[:, :])
                    last.then_inc(ffn.hT_ps.sem, 1)
                if back:
                    for s in range(2):
                        e = pe.value_load(experts[0:1, s, expert_of(m)], min_val=0, max_val=E - 1)
                        if s == 0:
                            need(pe, ffn.y_add, shift(m, -1), 1)
                        need(pe, ffn.aT, m, s + 1)
                        for c in range(KC):
                            last = nc.tensor.matmul(ps[:, 6, :], aT[:, s, c, :], w2_sb[:, e, c, :],
                                                    start=(s == 0 and c == 0), stop=(s == 1 and c == KC - 1))
                    last.then_inc(ffn.y_ps.sem, 1)
                if front:
                    for s in range(2):
                        e = pe.value_load(experts[0:1, s, expert_of(n)], min_val=0, max_val=E - 1)
                        if s == 0:
                            need(pe, ffn.hT, n, 1)
                        for c in range(KC):
                            nc.tensor.matmul(ps[:, 2 * i + s, :], hT[:, i, c, :], w1_sb[:, e, c, :],
                                             start=(c == 0), stop=False)
                        nc.tensor.matmul(ps[:, 2 * i + s, :], ones16[0:65, :],
                                         bias1[0:65, e, :], start=False, stop=True).then_inc(ffn.pre.sem, 1)

            def expert_of(n):
                if isinstance(n, Step):
                    b = n.var + n.add // 2
                    return bass.ds(b, 1)
                return slice(n // 2, n // 2 + 1)

            def ffn_pe(ffn, route):
                ffn_pe_step(ffn, 0, 0, False, True)
                ffn_pe_step(ffn, 1, 1, False, True)
                with pe.Fori(0, T // 2 - 1) as b:
                    for i in range(2):
                        ffn_pe_step(ffn, Step(b, 2, 2 + i), i, True, True)
                ffn_pe_step(ffn, T, 0, True, False)
                ffn_pe_step(ffn, T + 1, 1, True, False)

            pe.wait_ge(w12_in, 96)
            route_pe(route1)
            ffn_pe(ffn1, route1)
            if stop == 1:
                return

            def turn_weights():
                pe.wait_ge(mlp_w_in, 64)
                for u in range(3 * IC):
                    which, c = divmod(u, IC)
                    n = min(P, I - c * P)
                    if which == 2 and c == 0:
                        pe.wait_ge(down_in, 16)
                    need(pe, mlp.kept, u - 6, 1)
                    for k in range(KC):
                        if which < 2:
                            last = nc.tensor.transpose(ps[:, u % 6, k * P:k * P + n],
                                                       (gate_raw, up_raw)[which][0:n, c, k * P:(k + 1) * P],
                                                       ident[0:n, 0:n])
                        else:
                            last = nc.tensor.transpose(ps[0:n, u % 6, k * P:(k + 1) * P],
                                                       down_raw[:, k, c * P:c * P + n], ident[:, :])
                    last.then_inc(mlp.turned.sem, 1)

            def wide(first_bank, n_hT, w, signal):
                for q in range(0, I, D):
                    m = min(D, I - q)
                    for c in range(KC):
                        last = nc.tensor.matmul(ps[:, first_bank + q // D, 0:m], hT[:, n_hT, c, :], w[:, c, q:q + m],
                                                start=(c == 0), stop=(c == KC - 1))
                last.then_inc(signal.sem, 1)

            def mlp_turn_row(n, i):
                need(pe, mlp.row, n, 1)
                for c in range(KC):
                    last = nc.tensor.transpose(ps[:, ROW_BANK, c * P:(c + 1) * P],
                                               h_cur[:, i, c * P:(c + 1) * P], ident[:, :])
                last.then_inc(mlp.hT_ps.sem, 1)

            def mlp_gate(n, i):
                need(pe, mlp.hT, n, 1)
                need(pe, mlp.silu, shift(n, -1), 1)
                wide(0, i, wgT, mlp.gate)

            def mlp_pe_step(n, i, front):
                if front:
                    need(pe, mlp.prodT, shift(n, -1), 4)
                    mlp_turn_row(shift(n, 1), 1 - i)
                need(pe, mlp.prod, shift(n, -1), 3)
                need(pe, mlp.slow, shift(n, -1), SLOW)
                wide(3, i, wuT, mlp.up)
                need(pe, mlp.pick, n, PICKS)
                need(pe, mlp.y_add, shift(n, -1), 1)
                nc.tensor.matmul(check_ps, failed[:, :], ones32[:, 0:1], start=True, stop=True,
                                 skip_group_check=True).then_inc(mlp.check.sem, 1)
                if front:
                    mlp_gate(shift(n, 1), 1 - i)
                need(pe, mlp.prod, n, 3)
                need(pe, mlp.slow, n, SLOW)
                for k in range(3):
                    if k == 0 and front:
                        need(pe, mlp.hT, shift(n, 1), 1)
                    elif k == 2:
                        need(pe, mlp.prodT, n, 1)
                    for c in range(4 * k, min(4 * k + 4, IC)):
                        m = min(P, I - c * P)
                        last = nc.tensor.transpose(ps[0:m, PROD_BANK[k], (c - 4 * k) * P:(c - 4 * k + 1) * P],
                                                   mlp_prod[:, c * P:c * P + m], ident[:, :])
                    last.then_inc(mlp.prodT_ps.sem, 1)
                for c in range(IC):
                    m = min(P, I - c * P)
                    if c == 0:
                        need(pe, mlp.prodT, n, 2)
                    elif c == 8:
                        need(pe, mlp.prodT, n, 3)
                    elif c == IC - 1:
                        need(pe, mlp.prodT, n, 4)
                    last = nc.tensor.matmul(ps[:, Y_BANK, :], prodT[0:m, c, :], wdT[0:m, c, :],
                                            start=(c == 0), stop=(c == IC - 1))
                last.then_inc(mlp.y_ps.sem, 1)

            turn_weights()
            need(pe, mlp.kept, 3 * IC - 1, 1)
            need(pe, ffn1.y_add, T - 1, 1)
            mlp_turn_row(0, 0)
            mlp_gate(0, 0)
            mlp_pe_step(0, 0, True)
            mlp_pe_step(1, 1, True)
            with pe.Fori(0, T // 2 - 2) as b:
                for i in range(2):
                    mlp_pe_step(Step(b, 2, 2 + i), i, True)
            mlp_pe_step(T - 2, 0, True)
            mlp_pe_step(T - 1, 1, False)
            if stop == 2:
                return
            pe.wait_ge(w12_in2, 48)
            route_pe(route2)
            ffn_pe(ffn2, route2)


_INS = ["L0_attn_a_hidden_states", "L0_attn_a_w_attn", "L0_attn_a_b_attn", "L0_attn_a_w_proj", "L0_attn_a_b_proj",
        "L0_attn_b_w_gate", "L0_attn_b_w_up", "L0_attn_b_w_down", "L0_ffn_gate_w", "L0_ffn_gate_b",
        "L0_ffn_w1", "L0_ffn_b1", "L0_ffn_w2", "L0_ffn_b2"]


def kernel(**inputs):
    import concourse.bacc as bacc
    from concourse.bass_utils import run_bass_kernel_spmd

    nc = bacc.Bacc("TRN2", target_bir_lowering=False, num_devices=1)
    arrays = {f"in_{name}": np.ascontiguousarray(inputs[name]) for name in _INS}
    B, S, D = arrays["in_" + _INS[0]].shape
    arrays["k_alibi"], arrays["q_alibi"] = alibi_rows(32, S)
    args = [nc.dram_tensor(n, a.shape, mybir.dt.from_np(a.dtype), kind="ExternalInput").ap()
            for n, a in arrays.items()]
    out = nc.dram_tensor("out", (B, S, D), F32, kind="ExternalOutput").ap()
    build(nc, *args, out)
    r = run_bass_kernel_spmd(nc, [arrays], core_ids=[0])
    return r.results[0]["out"]
```

```python
from contextlib import ExitStack

import numpy as np

import concourse.bass as bass
from concourse import mybir

F32 = mybir.dt.float32
F32R = mybir.dt.float32r
BF16 = mybir.dt.bfloat16
U16 = mybir.dt.uint16
I32 = mybir.dt.int32
ALU = mybir.AluOpType
ACT = mybir.ActivationFunctionType
AX = mybir.AxisListType

P = 128
NEG = -1.0e30
EPS = 1e-5

TERMS = [(0, 0), (0, 1), (1, 0), (1, 1), (0, 2), (2, 0)]
BIAS_PARTS = 4
MAX_PARTS = 3


class Step:

    def __init__(self, var, mul, add):
        self.var, self.mul, self.add = var, mul, add

    def index(self):
        return self.var * self.mul + self.add


class Signal:

    def __init__(self, sem, per, credit, waited):
        self.sem, self.per, self.credit, self.waited = sem, per, credit, waited

    def count(self, step, k):
        if isinstance(step, Step):
            return step.var * (step.mul * self.per) + (step.add * self.per + k + self.credit)
        return step * self.per + (k + self.credit)


def need(eng, signal, step, k):
    if isinstance(step, int) and signal.count(step, k) <= 0:
        return
    eng.wait_ge(signal.sem, signal.count(step, k))


def need_apart(eng, signal, step, k):
    need(eng, signal, step, k)
    if not isinstance(step, int):
        eng.sem_inc(signal.waited, 1)


def shift(step, n):
    return Step(step.var, step.mul, step.add + n) if isinstance(step, Step) else step + n


class NormSignals:

    def __init__(self, sig, name):
        self.stat = sig(name + "_stat", 2)
        self.rstd = sig(name + "_rstd", 2)
        self.rows = sig(name + "_rows", 1)


class RouteSignals:

    def __init__(self, sig, name, E):
        self.logit = sig(name + "_logit", E, credit=1)
        self.mag = sig(name + "_mag", 1, credit=1)
        self.sums = sig(name + "_sums", 1)
        self.shifted = sig(name + "_shifted", 1)
        self.exp = sig(name + "_exp", 1)
        self.rank = sig(name + "_rank", 1)
        self.spread = sig(name + "_spread", 1)
        self.chain = sig(name + "_chain", 0)
        self.coef = sig(name + "_coef", 1)


class FFNSignals:

    def __init__(self, sig, name, E, split):
        self.split = split
        if split:
            self.hT_low = sig(name + "_hT_low", 1)
            self.aT_low = sig(name + "_aT_low", 2)
        self.row = sig(name + "_row", 1)
        self.hT_ps = sig(name + "_hT_ps", 1)
        self.hT = sig(name + "_hT", 1)
        self.pre = sig(name + "_pre", 2)
        self.fun = sig(name + "_fun", 6)
        self.mix = sig(name + "_mix", 8)
        self.aT_ps = sig(name + "_aT_ps", 2)
        self.aT = sig(name + "_aT", 2)
        self.y_ps = sig(name + "_y_ps", 1)
        self.y_add = sig(name + "_y_add", 1, credit=1)
        self.b2_add = sig(name + "_b2_add", E)


class MLPSignals:

    def __init__(self, sig, picks, slow):
        self.turned = sig("mlp_turned", 1)
        self.kept = sig("mlp_kept", 1)
        self.row = sig("mlp_row", 1)
        self.hT_ps = sig("mlp_hT_ps", 1)
        self.hT = sig("mlp_hT", 1)
        self.gate = sig("mlp_gate", 1)
        self.up = sig("mlp_up", 1)
        self.silu = sig("mlp_silu", 1)
        self.size = sig("mlp_size", 1)
        self.pick = sig("mlp_pick", picks)
        self.check = sig("mlp_check", 1)
        self.prod = sig("mlp_prod", 3)
        self.slow = sig("mlp_slow", slow)
        self.prodT_ps = sig("mlp_prodT_ps", 3)
        self.prodT = sig("mlp_prodT", 4)
        self.y_ps = sig("mlp_y_ps", 1)
        self.y_add = sig("mlp_y_add", 1, credit=1)


def index(step):
    return step.index() if isinstance(step, Step) else step


def tile_step(b, j, tiles):
    return b * tiles + j if isinstance(b, int) else Step(b, tiles, j)


def alibi_slopes(n):
    base = 2 ** (-2 ** (-(np.log2(n) - 3)))
    return (base ** np.arange(1, n + 1, dtype=np.float32)).astype(np.float32)


def bf16_parts(a, n):
    out = []
    for _ in range(n):
        top = (a.astype(np.float32).view(np.uint32) & 0xFFFF0000).view(np.float32)
        out.append((top.view(np.uint32) >> 16).astype(np.uint16))
        a = a - top.astype(np.float64)
    return out


def alibi_rows(H, S):
    ramp = alibi_slopes(H).astype(np.float64)[:, None] * np.arange(S, dtype=np.float64)[None, :]
    one = np.full((H, S), 0x3F80, np.uint16)
    k_rows, q_rows = [], []
    for kp, qp in zip(bf16_parts(ramp, BIAS_PARTS), bf16_parts(-ramp, BIAS_PARTS)):
        k_rows += [kp, one]
        q_rows += [one, qp]
    k_rows += [one] * MAX_PARTS
    return np.stack(k_rows), np.stack(q_rows)


def build(nc, x_in, w_attn, b_attn, w_proj, b_proj, w_gate, w_up, w_down,
          gate_w, gate_b, w1_in, b1_in, w2_in, b2_in, k_alibi, q_alibi, out):
    B, S, D = x_in.shape
    H = k_alibi.shape[1]
    HD = D // H
    KC = D // P
    T = B * S // P
    TB = S // P
    E = w1_in.shape[0]
    I = w_gate.shape[0]
    IC = (I + P - 1) // P
    G = 4
    NG = H // G
    HT = D // P
    TROWS = len(TERMS) * HD
    SROWS = TROWS + 2 * BIAS_PARTS
    MROWS = SROWS + MAX_PARTS
    SCALE = 1.0 / HD
    KEEP = I - I // 2
    BITS = 31
    PROBES, FIRST_GUESS, STEP, AIM = 4, 0.78, 0.0011, KEEP - 8
    VISION = int(S * 0.3)
    assert TB == 2 and D == 512

    with ExitStack() as ctx:
        def sem(name):
            return ctx.enter_context(nc.semaphore(name))

        waits = sem("waits")

        def sig(name, per, credit=0):
            return Signal(sem(name), per, credit, waits)

        at = [32 * ((nc.sbuf_base + 31) // 32)]

        def sb(name, shape, dt, offset=None):
            size = {F32: 4, F32R: 4, I32: 4, BF16: 2, U16: 2}[dt]
            n = size
            for s in shape[1:]:
                n *= s
            if offset is None:
                offset = at[0]
                at[0] += 32 * ((n + 31) // 32)
                assert at[0] <= nc.sbuf_usable_end, (name, at[0])
            return nc.alloc_sbuf_tensor_at(name, shape, dt, offset=offset)

        x_sb = sb("x_sb", [P, T, D], F32)
        h_sb_at = at[0]
        h_sb = sb("h_sb", [P, TB, D], F32)
        ident = sb("ident", [P, P], F32)
        ident16 = sb("ident16", [P, P], BF16)
        ones16 = sb("ones16", [P, P], BF16)
        neg_half = sb("neg_half", [P, TB], F32)
        stats = sb("stats", [P, TB, 6], F32)
        moments = sb("moments", [P, TB, 2], F32)
        spread = sb("spread", [P, TB], F32)
        rstd = sb("rstd", [P, TB], F32)
        NBIAS = 3 * D + D + E * D
        bias3 = sb("bias3", [P, NBIAS], BF16)
        B_ATTN, B_PROJ, B_1 = 0, 3 * D, 4 * D

        h_all = sb("h_all", [P, T, D], F32)
        ln_stats = sb("ln_stats", [P, 6], F32)
        ln_moments = sb("ln_moments", [P, 2], F32)
        ln_spread = sb("ln_spread", [P, 1], F32)
        ln_rstd = sb("ln_rstd", [P, 1], F32)
        logits = sb("logits", [P, T, E], F32)
        abs_sum = sb("abs_sum", [P, T], F32)
        gate_row = sb("gate_row", [P, (D + 1) * E], F32)
        gate_bias = sb("gate_bias", [P, E], F32)
        b2_row = sb("b2_row", [P, E, D], F32)
        junk = sb("junk", [P, D], F32)
        abs_junk = sb("abs_junk", [P, D], BF16)
        vision = sb("vision", [P, P], F32)
        text = sb("text", [P, P], F32)
        ones32 = sb("ones32", [P, P], F32)
        first_row = sb("first_row", [P, P], BF16)
        coef = sb("coef", [P, 2, T, E], F32)
        coef_b2 = sb("coef_b2", [P, T, E], F32)
        experts = sb("experts", [P, 2, B], I32)
        tiny = sb("tiny", [P, 21, T * E], F32)
        bits = sb("bits", [P, BITS], I32)
        cut_at = sb("cut_at", [P, 1], I32)
        cut_try = sb("cut_try", [P, 1], I32)
        cut_add = sb("cut_add", [P, 1], I32)
        cut_count = sb("cut_count", [P, 1], F32)
        surplus = sb("surplus", [P, 1], F32)
        guess = sb("guess", [P, 1], F32)
        guess_step = sb("guess_step", [P, 1], F32)
        threshold = sb("threshold", [P, 1], F32)
        size_sum = sb("size_sum", [P, 1], F32)
        short = sb("short", [P, 1], F32)
        failed = sb("failed", [P, 1], F32)
        failures = sb("failures", [P, 1], I32)
        ladder = sb("ladder", [P, 1 + 2 * 8], F32)
        numbers = sb("numbers", [P, 1 + 2 * 8], F32)
        pickout = sb("pickout", [P, 1 + 2 * 8], F32)

        arena = at[0]
        wqkv = sb("wqkv", [P, KC, 3 * D], F32)
        qk_tok = sb("qk_tok", [P, TB, 2 * D], F32)
        parts = sb("parts", [P, 2, 2, 3, HT // 2, S], BF16)
        resid = sb("resid", [P, 2, 2 * S], F32)
        gathered_end = at[0]
        wproj = sb("wproj", [P, KC, D], F32)
        actT = sb("actT", [P, KC, S], F32)
        qst = sb("qst", [P, H, S], BF16)
        kst = sb("kst", [P, H, S], BF16)
        v_stage = sb("v_stage", [P, TB, D], F32)
        v_ones = sb("v_ones", [P, TB, H, 2 * HD], F32)
        probs_at = at[0]
        probsT = sb("probsT", [P, 2, 3 * D], F32)
        outT = sb("outT", [P, 2, S], F32)
        o_tok = sb("o_tok", [P, TB, D], F32)
        rden = sb("rden", [P, 2, TB * G], F32)
        maskS = sb("maskS", [P, P], BF16)
        maskT = sb("maskT", [P, P], BF16)
        nmax = sb("nmax", [P, TB, H], F32)
        nmax_r = sb("nmax_r", [P, TB, H], F32)
        nmax_p = sb("nmax_p", [P, TB, MAX_PARTS, H], BF16)
        nmaxT = sb("nmaxT", [P, S], BF16)

        b_raw = sb("b_raw", [P, NBIAS], F32)
        b_p1 = sb("b_p1", [P, NBIAS], BF16, probs_at)
        b_p2 = sb("b_p2", [P, NBIAS], BF16, probs_at + 2 * NBIAS)

        at[0] = arena
        w1_sb = sb("w1_sb", [P, E, KC, D], F32)
        w2_sb = sb("w2_sb", [P, E, KC, D], F32)
        assert at[0] <= gathered_end
        ffn_at = at[0]
        h_cur = sb("h_cur", [P, 2, D], F32)
        hT = sb("hT", [P, 2, KC, P], F32, h_sb_at)
        funs = sb("funs", [P, 2, 3, D], F32)
        act_tok = sb("act_tok", [P, 2, 2, D], F32)
        aT = sb("aT", [P, 2, KC, P], F32)
        weights_at = max(at[0], ffn_at + 8 * D + 14 * I + 4 * IC * P + 128)
        weights_at = 32 * ((weights_at + 31) // 32)
        region = [weights_at + i * 4 * IC * D for i in range(3)]
        assert weights_at + 12 * IC * D <= nc.sbuf_usable_end
        wgT = sb("wgT", [P, KC, I], F32, region[0])
        wuT = sb("wuT", [P, KC, I], F32, region[1])
        wdT = sb("wdT", [P, IC, D], F32, region[2])
        gate_raw = sb("gate_raw", [P, IC, D], F32, region[1])
        up_raw = sb("up_raw", [P, IC, D], F32, region[2])
        down_raw = sb("down_raw", [P, KC, I], F32, arena)
        assert 4 * KC * I <= 4 * E * KC * D
        w1_hi = sb("w1_hi", [P, E, KC, D], F32R, weights_at)
        w1_lo = sb("w1_lo", [P, E, KC, D], F32R, arena)
        w2_hi = sb("w2_hi", [P, E, KC, D], F32R, weights_at + 4 * E * KC * D)
        w2_lo = sb("w2_lo", [P, E, KC, D], F32R, arena + 4 * E * KC * D)
        split_at = weights_at + 8 * E * KC * D
        hT_hi, hT_lo, aT_hi, aT_lo = [sb(name, [P, 2, KC, P], F32R, split_at + i * 8 * KC * P)
                                      for i, name in enumerate(("hT_hi", "hT_lo", "aT_hi", "aT_lo"))]
        assert split_at + 32 * KC * P <= nc.sbuf_usable_end
        at[0] = ffn_at + 8 * D
        mlp_s = sb("mlp_s", [P, I], F32)
        mlp_size = sb("mlp_size", [P, I], F32)
        mlp_prod = sb("mlp_prod", [P, I], F32)
        mlp_flag = sb("mlp_flag", [P, I], BF16)
        prodT = sb("prodT", [P, IC, P], F32)
        assert at[0] <= region[0]

        ps = ctx.enter_context(nc.psum_tensor("ps", [P, 8, 512], F32))

        x_first, x_rest = sem("x_first"), sem("x_rest")
        wqkv_in = [sem(f"wqkv_in{c}") for c in range(KC)]
        wproj_in, alibi_in, bias_in = sem("wproj_in"), sem("alibi_in"), sem("bias_in")
        consts, ident_ok, bits_set = sem("consts"), sem("ident_ok"), sem("bits_set")
        bias_cut, bias_zero, bias_in2 = sem("bias_cut"), sem("bias_zero"), sem("bias_in2")
        stat = sig("stat", 2 * TB)
        rstd_ok = sig("rstd_ok", 2)
        h_ok = sig("h_ok", TB)
        hT_ps = sig("hT_ps", TB)
        hT_ok = sig("hT_ok", TB)
        qkv_ps = sig("qkv_ps", 3 * TB)
        qv_out = sig("qv_out", 2 * TB)
        k_out = sig("k_out", TB)
        tr_ps = sig("tr_ps", 4)
        part1 = sig("part1", 4)
        res1 = sig("res1", 4)
        part2 = sig("part2", 4)
        part3 = sig("part3", 4)
        cuts_out = [sig(f"cuts_out{half}", 16 * 2) for half in range(2)]
        scat = [sig(f"scat{half}", 16 * 2 * len(TERMS)) for half in range(2)]
        GHALF = NG // 2
        v_copy = sig("v_copy", 1)
        s_ps = sig("s_ps", NG)
        max_ok = sig("max_ok", 2 * NG)
        nm_cut = sig("nm_cut", 4)
        nmT_ps = sig("nmT_ps", 1)
        nmT_ok = sig("nmT_ok", 1)
        nm_in = sig("nm_in", 16 * MAX_PARTS)
        sT_ps = sig("sT_ps", NG)
        exp_ok = sig("exp_ok", NG)
        pv_ps = sig("pv_ps", NG)
        outT_ok = sig("outT_ok", NG)
        oTr_ps = sig("oTr_ps", NG)
        rden_ok = sig("rden_ok", NG)
        norm_ok = sig("norm_ok", NG)
        oT_ps = sig("oT_ps", TB)
        oT_ok = sig("oT_ok", TB)
        y_ps = sig("y_ps", TB)
        x_add = sig("x_add", TB, credit=TB)

        norm2, norm3, norm4 = NormSignals(sig, "norm2"), NormSignals(sig, "norm3"), NormSignals(sig, "norm4")
        route1, route2 = RouteSignals(sig, "route1", E), RouteSignals(sig, "route2", E)
        ffn1, ffn2 = FFNSignals(sig, "ffn1", E, False), FFNSignals(sig, "ffn2", E, True)
        SLOW = 1 + 4 * BITS + 8
        PICKS = 1 + 3 * (PROBES - 1) + 10
        mlp = MLPSignals(sig, PICKS, SLOW)
        gate_in, w1_here, w2_here = sem("gate_in"), sem("w1_here"), sem("w2_here")
        w1_high, w1_low, w2_high, w2_low = sem("w1_high"), sem("w1_low"), sem("w2_high"), sem("w2_low")
        mlp_w_in, down_in, w1_back = sem("mlp_w_in"), sem("down_in"), sem("w1_back")
        out_done = sem("out_done")

        cuts = nc.dram_tensor("cuts", (2, 2, 3, D // 2, S), BF16, kind="Internal").ap()
        x_v = x_in.rearrange("b (j p) d -> p (b j) d", p=P)
        out_v = out.rearrange("b (j p) d -> p (b j) d", p=P)

        gate_v = gate_row[:, :].rearrange("p (d e) -> p d e", e=E)
        bias1 = bias3[:, B_1:B_1 + E * D].rearrange("p (e n) -> p e n", e=E)
        slot = [ps[:, 0:3, :], ps[:, 3:6, :]]
        work = [ps[:, 6, :], ps[:, 7, :]]

        ROW_BANK, CHECK_BANK, PROD_BANK, Y_BANK = 6, 7, (6, 7, 6), 7
        gate_ps = ps[:, 0:3, :].rearrange("p b n -> p (b n)")[:, 0:I]
        check_ps = ps[0:1, CHECK_BANK, 0:1]
        up_ps = ps[:, 3:6, :].rearrange("p b n -> p (b n)")[:, 0:I]

        def send_maxima(eng, b):
            need(eng, nmT_ok, b, 1)
            for m in range(MAX_PARTS):
                eng.dma_start(qst[SROWS + m:SROWS + m + 1, :, :],
                              nmaxT[m * H:(m + 1) * H, :]).then_inc(nm_in.sem, 16)

        block = ctx.enter_context(nc.Block())

        @block.sync
        def _(sp):
            sp.dma_start(x_sb[:, 0:TB, :], x_v[:, 0:TB, :]).then_inc(x_first, 16)
            sp.wait_ge(bias_zero, 1)
            for i in range(3):
                sp.dma_start(b_raw[32 * i:32 * i + 1, B_ATTN:B_ATTN + 3 * D],
                             b_attn.rearrange("(a n) -> a n", a=1)).then_inc(bias_in, 16)
            wa = w_attn.rearrange("(c p) n -> p c n", p=P)
            for c in range(KC):
                sp.dma_start(wqkv[:, c, :], wa[:, c, :]).then_inc(wqkv_in[c], 16)
            sp.dma_start(x_sb[:, TB:T, :], x_v[:, TB:T, :]).then_inc(x_rest, 16)
            sp.dma_start(kst[TROWS:MROWS, :, :].bitcast(U16), k_alibi).then_inc(alibi_in, 16)
            sp.dma_start(qst[TROWS:SROWS, :, :].bitcast(U16), q_alibi).then_inc(alibi_in, 16)
            sp.dma_start(gate_row[:, :], gate_w.rearrange("d e -> (d e)").partition_broadcast(P)).then_inc(gate_in, 16)
            sp.dma_start(gate_bias[:, :], gate_b.partition_broadcast(P)).then_inc(gate_in, 16)
            sp.dma_start(b2_row[:, :, :].rearrange("p e n -> p (e n)"),
                         b2_in.rearrange("e n -> (e n)").partition_broadcast(P)).then_inc(gate_in, 16)
            sp.dma_start(wproj[:, :, :], w_proj.rearrange("(c p) n -> p c n", p=P)).then_inc(wproj_in, 16)

            def gather(b, before):
                for half in range(2):
                    for side in range(2):
                        need(sp, part3, b, 2 * half + side + 1)
                        sp.dma_start(cuts[side, half].rearrange("m (g p) t -> p (m g) t", p=P),
                                     parts[:, side, half].rearrange("p m g t -> p (m g) t")
                                     ).then_inc(cuts_out[half].sem, 16)
                    need(sp, sT_ps, before, (half + 1) * GHALF)
                    need(sp, cuts_out[half], b, 16 * 2)
                    hs = slice(half * H // 2, (half + 1) * H // 2)
                    for side, stack in enumerate((qst, kst)):
                        for t, term in enumerate(TERMS):
                            sp.dma_start(
                                stack[HD * t:HD * t + HD, hs, :],
                                cuts[side, half, term[1 - side]].rearrange("(h d) t -> d h t", d=HD),
                            ).then_inc(scat[half].sem, 16)

            gather(0, -1)
            with sp.Fori(0, B - 1) as b:
                send_maxima(sp, b)
                gather(b + 1, b)

            need(sp, qkv_ps, B - 1, 3 * TB)
            for half in range(2):
                need(sp, scat[half], B - 1, scat[half].per)
            for e in range(E):
                sp.dma_start(w1_sb[:, e], w1_in[e].rearrange("(c p) n -> p c n", p=P)).then_inc(w1_here, 16)
            for e in range(E):
                sp.dma_start(w2_sb[:, e], w2_in[e].rearrange("(c p) n -> p c n", p=P)).then_inc(w2_here, 16)

            need(sp, y_ps, B - 1, TB)
            full = I // P * P
            for raw, w in ((gate_raw, w_gate), (up_raw, w_up)):
                sp.dma_start(raw[:, 0:I // P, :], w[0:full].rearrange("(c p) n -> p c n", p=P)).then_inc(mlp_w_in, 16)
                if full < I:
                    sp.dma_start(raw[0:I - full, I // P, :], w[full:I]).then_inc(mlp_w_in, 16)

            need(sp, ffn1.pre, T - 1, 2)
            sp.dma_start(down_raw[:, :, :], w_down.rearrange("(c p) n -> p c n", p=P)).then_inc(down_in, 16)
            need(sp, mlp.turned, 3 * IC - 1, 1)
            for e in range(E):
                sp.dma_start(w1_sb[:, e], w1_in[e].rearrange("(c p) n -> p c n", p=P)).then_inc(w1_back, 16)
            for n in range(T):
                need(sp, ffn2.b2_add, n, E)
                sp.dma_start(out_v[:, n, :], x_sb[:, n, :]).then_inc(out_done, 16)
            sp.wait_ge(out_done, 16 * T)

        @block.gpsimd
        def _(pool):
            nc.gpsimd.memset(ident[:, :], 0.0).then_inc(ident_ok, 1)
            nc.gpsimd.memset(neg_half[:, :], -0.5).then_inc(ident_ok, 1)
            pool.wait_ge(ident_ok, 2)
            nc.gpsimd.affine_select(out=ident[:, :], in_=ident[:, :], compare_op=ALU.not_equal, fill=1.0,
                                    base=0, pattern=[[-1, P]], channel_multiplier=1).then_inc(ident_ok, 1)
            nc.gpsimd.memset(ones16[:, :], 1.0).then_inc(ident_ok, 1)

            def constants():
                nc.gpsimd.memset(maskS[:, :], 0.0).then_inc(consts, 1)
                nc.gpsimd.memset(maskT[:, :], 0.0).then_inc(consts, 1)
                nc.gpsimd.memset(vision[:, :], 1.0).then_inc(consts, 1)
                nc.gpsimd.memset(ones32[:, :], 1.0).then_inc(consts, 1)
                nc.gpsimd.memset(first_row[:, :], 1.0).then_inc(consts, 1)
                nc.gpsimd.memset(v_ones[:, :, :, HD:2 * HD], 1.0).then_inc(consts, 1)
                pool.wait_ge(ident_ok, 3)
                nc.gpsimd.tensor_copy(ident16[:, :], ident[:, :]).then_inc(consts, 1)
                pool.wait_ge(consts, 5)
                nc.gpsimd.affine_select(out=maskS[:, :], in_=maskS[:, :], compare_op=ALU.is_ge, fill=NEG,
                                        base=0, pattern=[[-1, P]], channel_multiplier=1).then_inc(consts, 1)
                nc.gpsimd.affine_select(out=maskT[:, :], in_=maskT[:, :], compare_op=ALU.is_ge, fill=NEG,
                                        base=0, pattern=[[1, P]], channel_multiplier=-1).then_inc(consts, 1)
                nc.gpsimd.affine_select(out=vision[:, :], in_=vision[:, :], compare_op=ALU.is_ge, fill=0.0,
                                        base=VISION - 1, pattern=[[0, P]], channel_multiplier=-1).then_inc(consts, 1)
                nc.gpsimd.affine_select(out=first_row[:, :], in_=first_row[:, :], compare_op=ALU.is_ge, fill=0.0,
                                        base=0, pattern=[[0, P]], channel_multiplier=-1).then_inc(consts, 1)
                pool.wait_ge(consts, 10)
                nc.gpsimd.tensor_tensor(text[:, :], ones32[:, :], vision[:, :], ALU.subtract).then_inc(consts, 1)
                for i in range(1 + 2 * 8):
                    nc.gpsimd.memset(numbers[:, i:i + 1], float(i)).then_inc(bits_set, 1)
                for i in range(BITS):
                    nc.gpsimd.memset(bits[:, i:i + 1], 1 << (BITS - 1 - i)).then_inc(bits_set, 1)

            def ln(b):
                need_apart(pool, stat, b, 2 * TB)
                nc.gpsimd.tensor_scalar(spread[:, :], moments[:, :, 1], EPS, None, ALU.add).then_inc(rstd_ok.sem, 1)
                need(pool, rstd_ok, b, 1)
                nc.gpsimd.tensor_tensor(rstd[:, :], spread[:, :], neg_half[:, :], ALU.pow).then_inc(rstd_ok.sem, 1)

            def cut(b):
                for f in range(4):
                    side, pair = f % 2, f // 2
                    need(pool, part2, b, f + 1)
                    r = resid[:, f % 2, :].rearrange("p (h t) -> p h t", h=2)
                    nc.gpsimd.tensor_tensor(parts[:, side, pair, 2, :, :], r,
                                            parts[:, side, pair, 1, :, :], ALU.subtract
                                            ).then_inc(part3.sem, 1)

            def values(b):
                need(pool, qv_out, b, 2 * TB)
                need_apart(pool, pv_ps, b - 1, NG)
                nc.gpsimd.tensor_copy(v_ones[:, :, :, 0:HD],
                                      v_stage[:, :, :].rearrange("p j (h d) -> p j h d", d=HD)).then_inc(v_copy.sem, 1)

            def norm(signals, step):
                need_apart(pool, signals.stat, step, 2)
                nc.gpsimd.tensor_scalar(ln_spread[:, :], ln_moments[:, 1:2], EPS, None,
                                        ALU.add).then_inc(signals.rstd.sem, 1)
                need(pool, signals.rstd, step, 1)
                nc.gpsimd.tensor_tensor(ln_rstd[:, :], ln_spread[:, :], neg_half[:, 0:1],
                                        ALU.pow).then_inc(signals.rstd.sem, 1)

            ln(0)
            constants()
            cut(0)
            values(0)
            ln(1)
            cut(1)
            values(1)
            with pool.Fori(0, B - 2) as b:
                ln(b + 2)
                cut(b + 2)
                for j in range(TB):
                    norm(norm2, tile_step(b, j, TB))
                values(b + 2)
            for b in (B - 2, B - 1):
                for j in range(TB):
                    norm(norm2, tile_step(b, j, TB))

            def take_row(ffn, n, i, before):
                need(pool, before.rows, n, 1)
                need_apart(pool, ffn.hT_ps, shift(n, -2), 1)
                nc.gpsimd.tensor_copy(h_cur[:, i, :], h_all[:, index(n), :]).then_inc(ffn.row.sem, 1)

            def ffn_pool(ffn, before, after):
                with pool.Fori(0, T // 2 - 1) as b:
                    for i in range(2):
                        take_row(ffn, Step(b, 2, 2 + i), i, before)
                        if after is not None:
                            norm(after, Step(b, 2, i))
                if after is not None:
                    for n in range(T - 2, T):
                        norm(after, n)

            for n in range(2):
                take_row(ffn1, n, n, norm2)
            ffn_pool(ffn1, norm2, norm3)
            for n in range(2):
                take_row(mlp, n, n, norm3)
            with pool.Fori(0, T // 2 - 1) as b:
                for i in range(2):
                    take_row(mlp, Step(b, 2, 2 + i), i, norm3)
                    norm(norm4, Step(b, 2, i))

            def weight_low(out, w, high, e, count, signal):
                pool.wait_ge(count, e + 1)
                nc.gpsimd.tensor_tensor(out[:, e], w[:, e], high[:, e].bitcast(F32), ALU.subtract).then_inc(signal, 1)

            weight_low(w1_lo, w1_sb, w1_hi, 0, w1_high, w1_low)
            norm(norm4, T - 2)
            for e in range(1, E):
                weight_low(w1_lo, w1_sb, w1_hi, e, w1_high, w1_low)
            norm(norm4, T - 1)
            for n in range(2):
                take_row(ffn2, n, n, norm4)
            for e in range(E):
                weight_low(w2_lo, w2_sb, w2_hi, e, w2_high, w2_low)
            ffn_pool(ffn2, norm4, None)

        @block.scalar
        def _(act):
            act.sem_inc(route1.mag.sem, 1)
            act.sem_inc(route2.mag.sem, 1)
            act.wait_ge(bias_zero, 1)
            for i in range(3):
                row = b_raw[32 * i:32 * i + 1]
                act.dma_start(row[:, B_PROJ:B_PROJ + D], b_proj.rearrange("(a n) -> a n", a=1)).then_inc(bias_in2, 16)
                act.dma_start(row[:, B_1:B_1 + E * D], b1_in.rearrange("(a e) n -> a (e n)", a=1)).then_inc(bias_in2, 16)

            def project(b):
                for j in range(TB):
                    need(act, hT_ps, b, j + 1)
                    nc.scalar.copy(actT[:, :, j * P:(j + 1) * P],
                                   work[j].rearrange("p (c t) -> p c t", c=KC)).then_inc(hT_ok.sem, 1)
                for j in range(TB):
                    need(act, qkv_ps, b, 3 * j + 1)
                    nc.scalar.mul(qk_tok[:, j, 0:D], work[j % 2], SCALE).then_inc(qv_out.sem, 1)
                    if j < TB - 1:
                        values(b, j)

            def values(b, j):
                need(act, qkv_ps, b, 3 * j + 3)
                nc.scalar.copy(v_stage[:, j, :], work[j % 2]).then_inc(qv_out.sem, 1)

            def maxima(b):
                need(act, nmT_ps, b, 1)
                nc.scalar.copy(nmaxT[0:MAX_PARTS * H, :],
                               work[0].bitcast(BF16)[0:MAX_PARTS * H, 0:S]).then_inc(nmT_ok.sem, 1)

            def cut(b, fs):
                for f in fs:
                    side, pair = f % 2, f // 2
                    need(act, tr_ps, b, f + 1)
                    nc.scalar.copy(parts[:, side, pair, 0, :, :],
                                   work[f % 2].rearrange("p (h t) -> p h t", h=2)).then_inc(part1.sem, 1)
                    if f >= 1:
                        second_part(b, f - 1)
                if 3 in fs:
                    second_part(b, 3)

            def second_part(b, f):
                side, pair = f % 2, f // 2
                need(act, res1, b, f + 1)
                nc.scalar.copy(parts[:, side, pair, 1, :, :],
                               resid[:, f % 2, :].rearrange("p (h t) -> p h t", h=2)).then_inc(part2.sem, 1)

            def attend(b):
                for g in range(NG):
                    need(act, sT_ps, b, g + 1)
                    if g >= 2:
                        need(act, pv_ps, b, g - 1)
                    nc.scalar.activation(probsT[:, g % 2, :].rearrange("p (k n) -> p k n", k=3), slot[g % 2],
                                         ACT.Exp).then_inc(exp_ok.sem, 1)
                for j in range(TB):
                    need(act, oT_ps, b, j + 1)
                    nc.scalar.copy(actT[:, :, j * P:(j + 1) * P],
                                   work[j].rearrange("p (c t) -> p c t", c=KC)).then_inc(oT_ok.sem, 1)

            def magnitudes(norm, route, step):
                need(act, norm.rows, step, 1)
                t = index(step)
                need(act, route.mag, shift(step, -1), 1)
                nc.scalar.activation(abs_junk[:, :], h_all[:, t, :], ACT.Abs,
                                     accum_out=abs_sum[:, bass.ds(t, 1)]).then_inc(route.mag.sem, 1)

            project(0)
            values(0, TB - 1)
            cut(0, range(4))
            with act.Fori(0, B - 1) as b:
                project(b + 1)
                cut(b + 1, (0,))
                values(b + 1, TB - 1)
                maxima(b)
                cut(b + 1, (1, 2, 3))
                attend(b)
            maxima(B - 1)
            send_maxima(act, B - 1)
            for t in range(T - 2 * TB):
                magnitudes(norm2, route1, t)
            attend(B - 1)
            for t in range(T - 2 * TB, T):
                magnitudes(norm2, route1, t)

            def route_act(route):
                need(act, route.shifted, 0, 1)
                nc.scalar.activation(tiny[:, 10, :], tiny[:, 0, :], ACT.Exp).then_inc(route.exp.sem, 1)

            def functions(ffn, n, i, s):
                need(act, ffn.pre, n, s + 1)
                need(act, ffn.mix, shift(n, -1), 4 * (s + 1))
                x = ps[:, 2 * i + s, :]
                nc.scalar.activation(funs[:, s, 0, :], x, ACT.Tanh).then_inc(ffn.fun.sem, 1)
                nc.scalar.activation(funs[:, s, 1, :], x, ACT.Gelu).then_inc(ffn.fun.sem, 1)
                nc.scalar.activation(funs[:, s, 2, :], x, ACT.Tanh, scale=0.5).then_inc(ffn.fun.sem, 1)

            def ffn_act_step(ffn, n, i, back, front, mid):
                if back:
                    for s in range(2):
                        need(act, ffn.aT_ps, shift(n, -2), s + 1)
                        nc.scalar.copy((aT_hi if ffn.split else aT)[:, s, :, :], ps[:, 4 + s, :].rearrange("p (c t) -> p c t", c=KC)
                                       ).then_inc(ffn.aT.sem, 1)
                if front:
                    need(act, ffn.hT_ps, n, 1)
                    nc.scalar.copy((hT_hi if ffn.split else hT)[:, i, :, :], ps[:, 7, :].rearrange("p (c t) -> p c t", c=KC)
                                   ).then_inc(ffn.hT.sem, 1)
                if mid:
                    functions(ffn, shift(n, -1), 1 - i, 1)
                if front:
                    functions(ffn, n, i, 0)

            def ffn_act(ffn):
                ffn_act_step(ffn, 0, 0, False, True, False)
                ffn_act_step(ffn, 1, 1, False, True, True)
                with act.Fori(0, T // 2 - 1) as b:
                    for i in range(2):
                        ffn_act_step(ffn, Step(b, 2, 2 + i), i, True, True, True)
                ffn_act_step(ffn, T, 0, True, False, True)
                ffn_act_step(ffn, T + 1, 1, True, False, False)

            route_act(route1)
            ffn_act(ffn1)

            def rows_of(u):
                return min(P, I - u % IC * P)

            for u in range(3 * IC):
                need(act, mlp.turned, u, 1)
                c, n = u % IC, rows_of(u)
                if u < 2 * IC:
                    nc.scalar.copy((wgT, wuT)[u // IC][:, :, c * P:c * P + n],
                                   ps[:, u % 6, :].rearrange("p (c t) -> p c t", c=KC)[:, :, 0:n]
                                   ).then_inc(mlp.kept.sem, 1)
                else:
                    nc.scalar.copy(wdT[0:n, c, :], ps[0:n, u % 6, :]).then_inc(mlp.kept.sem, 1)

            def gate_act(n, i):
                need(act, mlp.hT_ps, n, 1)
                nc.scalar.copy(hT[:, i, :, :], ps[:, ROW_BANK, :].rearrange("p (c t) -> p c t", c=KC)
                               ).then_inc(mlp.hT.sem, 1)

            def sizes(n):
                need(act, mlp.gate, n, 1)
                need(act, mlp.prod, shift(n, -1), 3)
                need(act, mlp.slow, shift(n, -1), SLOW)
                nc.scalar.activation(mlp_s[:, :], gate_ps, ACT.Silu).then_inc(mlp.silu.sem, 1)
                need(act, mlp.silu, n, 1)
                nc.scalar.activation(mlp_size[:, :], mlp_s[:, :], ACT.Abs,
                                     accum_out=size_sum[:, :]).then_inc(mlp.size.sem, 1)

            def mlp_act_step(n, i, back):
                gate_act(shift(n, 1), 1 - i)
                sizes(shift(n, 1))
                if back:
                    magnitudes(norm4, route2, shift(n, -1))

            gate_act(0, 0)
            sizes(0)
            mlp_act_step(0, 0, False)
            with act.Fori(0, T // 2 - 1) as b:
                for i in range(2):
                    mlp_act_step(Step(b, 2, 1 + i), 1 - i, True)

            def high_part(out, w, e, signal):
                nc.scalar.copy(out[:, e], w[:, e]).then_inc(signal, 1)

            act.wait_ge(w1_back, 48)
            need(act, mlp.gate, T - 1, 1)
            need(act, mlp.up, T - 1, 1)
            for e in range(E):
                high_part(w1_hi, w1_sb, e, w1_high)
            magnitudes(norm4, route2, T - 2)
            act.wait_ge(w2_here, 48)
            for e in range(E - 1):
                high_part(w2_hi, w2_sb, e, w2_high)
            need(act, mlp.y_ps, T - 1, 1)
            high_part(w2_hi, w2_sb, E - 1, w2_high)
            magnitudes(norm4, route2, T - 1)
            route_act(route2)
            ffn_act(ffn2)

        @block.vector
        def _(dve):
            def ln(b):
                for j in range(TB):
                    x = x_sb[:, b * TB + j, :]
                    nc.vector.bn_stats(stats[:, j, :], x).then_inc(stat.sem, 1)
                need_apart(dve, stat, b, TB)
                for j in range(TB):
                    nc.vector.bn_aggr(moments[:, j, :], stats[:, j, :]).then_inc(stat.sem, 1)
                need(dve, rstd_ok, b, 2)
                for j in range(TB):
                    nc.vector.tensor_scalar(h_sb[:, j, :], x_sb[:, b * TB + j, :], moments[:, j, 0:1],
                                            rstd[:, j:j + 1], ALU.subtract, ALU.mult).then_inc(h_ok.sem, 1)

            def keys(b, j):
                need(dve, qkv_ps, b, 3 * j + 2)
                nc.vector.tensor_copy(qk_tok[:, j, D:2 * D], work[1 - j % 2]).then_inc(k_out.sem, 1)

            def residues(b):
                for f in range(4):
                    side, pair = f % 2, f // 2
                    need(dve, part1, b, f + 1)
                    if f >= 2:
                        need(dve, part3, b, f - 1)
                    r = resid[:, f % 2, :].rearrange("p (h t) -> p h t", h=2)
                    nc.vector.tensor_tensor(r, work[f % 2].rearrange("p (h t) -> p h t", h=2),
                                            parts[:, side, pair, 0, :, :],
                                            ALU.subtract).then_inc(res1.sem, 1)

            def maxima(b, between):
                for g in range(NG):
                    need(dve, s_ps, b, g + 1)
                    sl = slot[g % 2]
                    nc.vector.tensor_reduce(nmax[:, 0, g * G:(g + 1) * G],
                                            sl[:, 0, :].rearrange("p (h k) -> p h k", h=G),
                                            AX.X, ALU.max, negate=True).then_inc(max_ok.sem, 1)
                    nc.vector.tensor_reduce(nmax[:, 1, g * G:(g + 1) * G],
                                            sl[:, 1:3, :].rearrange("p s (h k) -> p (s h) k", h=2),
                                            AX.X, ALU.max, negate=True).then_inc(max_ok.sem, 1)
                    between(g)
                need(dve, max_ok, b, 2 * NG)
                nc.vector.tensor_copy(nmax_p[:, :, 0, :], nmax[:, :, :]).then_inc(nm_cut.sem, 1)
                need(dve, nm_cut, b, 1)
                nc.vector.tensor_tensor(nmax_r[:, :, :], nmax[:, :, :], nmax_p[:, :, 0, :],
                                        ALU.subtract).then_inc(nm_cut.sem, 1)
                need(dve, nm_cut, b, 2)
                nc.vector.tensor_copy(nmax_p[:, :, 1, :], nmax_r[:, :, :]).then_inc(nm_cut.sem, 1)
                need(dve, nm_cut, b, 3)
                nc.vector.tensor_tensor(nmax_p[:, :, 2, :], nmax_r[:, :, :], nmax_p[:, :, 1, :],
                                        ALU.subtract).then_inc(nm_cut.sem, 1)

            def second_norm(b, j, part):
                t = tile_step(b, j, TB)
                if part == 0:
                    norm_stats(norm2, t)
                elif part == 1:
                    norm_rows(norm2, t)
                else:
                    logit_rows(norm2, route1, t)

            def attend(b, tail):
                def normalise(g):
                    need(dve, oTr_ps, b, g + 1)
                    o = work[g % 2][:, S:2 * S].rearrange("p (j h e) -> p j h e", j=TB, h=G)
                    nc.vector.reciprocal(rden[:, g % 2, :].rearrange("p (j h) -> p j h", j=TB),
                                         o[:, :, :, HD]).then_inc(rden_ok.sem, 1)
                    need(dve, rden_ok, b, g + 1)
                    r = rden[:, g % 2, :].rearrange("p (j h) -> p j h", j=TB).unsqueeze(3)
                    nc.vector.tensor_tensor(
                        o_tok[:, :, g * G * HD:(g + 1) * G * HD].rearrange("p j (h d) -> p j h d", h=G),
                        o[:, :, :, 0:HD], r.broadcast_to([P, TB, G, HD]), ALU.mult).then_inc(norm_ok.sem, 1)

                for g in range(NG):
                    need(dve, pv_ps, b, g + 1)
                    nc.vector.tensor_copy(outT[:, g % 2, :], work[g % 2][:, 0:S]).then_inc(outT_ok.sem, 1)
                    if g >= 1:
                        normalise(g - 1)
                    if tail and g < 2 * 3:
                        second_norm(b - 1, g // 3, g % 3)
                normalise(NG - 1)
                for j in range(TB):
                    need(dve, y_ps, b, j + 1)
                    x = x_sb[:, b * TB + j, :]
                    nc.vector.tensor_tensor(x, work[j], x, ALU.add).then_inc(x_add.sem, 1)

            def norm(signals, step):
                norm_stats(signals, step)
                norm_rows(signals, step)

            def norm_stats(signals, step):
                x = x_sb[:, index(step), :]
                nc.vector.bn_stats(ln_stats[:, :], x).then_inc(signals.stat.sem, 1)
                need_apart(dve, signals.stat, step, 1)
                nc.vector.bn_aggr(ln_moments[:, :], ln_stats[:, :]).then_inc(signals.stat.sem, 1)

            def norm_rows(signals, step):
                x = x_sb[:, index(step), :]
                need(dve, signals.rstd, step, 2)
                nc.vector.tensor_scalar(h_all[:, index(step), :], x, ln_moments[:, 0:1], ln_rstd[:, :],
                                        ALU.subtract, ALU.mult).then_inc(signals.rows.sem, 1)

            def logit_rows(norm, route, step):
                need(dve, norm.rows, step, 1)
                t = index(step)
                for e in range(E):
                    need(dve, route.logit, step, e)
                    nc.vector.scalar_tensor_tensor(out=junk[:, :], in0=h_all[:, t, :], scalar=1.0,
                                                   in1=gate_v[:, 0:D, e], op0=ALU.mult, op1=ALU.mult,
                                                   accum_out=logits[:, t, e:e + 1]).then_inc(route.logit.sem, 1)

            def cut_bias(lo, hi, n):
                r = t = b_raw[0:65, lo:hi]
                nc.vector.tensor_copy(b_p1[0:65, lo:hi], r).then_inc(bias_cut, 1)
                dve.wait_ge(bias_cut, n + 1)
                nc.vector.tensor_tensor(t, r, b_p1[0:65, lo:hi], ALU.subtract).then_inc(bias_cut, 1)
                dve.wait_ge(bias_cut, n + 2)
                nc.vector.tensor_copy(b_p2[0:65, lo:hi], t).then_inc(bias_cut, 1)
                nc.vector.tensor_copy(bias3[0:1, lo:hi], b_p1[0:1, lo:hi]).then_inc(bias_cut, 1)
                dve.wait_ge(bias_cut, n + 3)
                nc.vector.tensor_copy(bias3[32:33, lo:hi], b_p2[32:33, lo:hi]).then_inc(bias_cut, 1)
                nc.vector.tensor_tensor(bias3[64:65, lo:hi], t[64:65], b_p2[64:65, lo:hi],
                                        ALU.subtract).then_inc(bias_cut, 1)

            nc.vector.memset(b_raw[0:65, :], 0.0).then_inc(bias_zero, 1)
            nc.vector.memset(bias3[0:65, :], 0.0).then_inc(bias_zero, 1)
            dve.sem_inc(x_add.sem, TB)
            dve.sem_inc(route1.logit.sem, 1)
            dve.sem_inc(route2.logit.sem, 1)
            dve.wait_ge(x_first, 16)
            ln(0)
            dve.wait_ge(bias_in, 48)
            dve.wait_ge(bias_zero, 2)
            cut_bias(B_ATTN, B_ATTN + 3 * D, 0)
            for j in range(TB):
                keys(0, j)
            residues(0)
            dve.wait_ge(bias_in2, 96)
            cut_bias(B_PROJ, NBIAS, 6)
            dve.wait_ge(x_rest, 16)
            dve.wait_ge(gate_in, 48)
            def step(b, tail):
                ln(b + 1)
                maxima(b, lambda g: keys(b + 1, (g - 3) // 3) if g in (3, 6) else None)
                residues(b + 1)
                attend(b, tail)

            step(0, False)
            with dve.Fori(0, B - 2) as b:
                step(b + 1, True)
            maxima(B - 1, lambda g: None)
            attend(B - 1, True)
            dve.wait_ge(x_add.sem, x_add.count(B - 1, TB))
            for j, part in ((0, 0), (0, 1), (1, 0), (0, 2), (1, 1), (1, 2)):
                second_norm(B - 1, j, part)

            def route_dve(route):
                done = [0]

                def link(ins):
                    done[0] += 1
                    ins.then_inc(route.chain.sem, 1)
                    dve.wait_ge(route.chain.sem, done[0])

                def row(i, n):
                    return tiny[:, i, 0:n]

                tt, ts = nc.vector.tensor_tensor, nc.vector.tensor_scalar
                need(dve, route.logit, T - 1, E)
                need(dve, route.sums, 0, 1)
                ratio, vis = row(3, B), row(4, B)
                link(ts(vis, ps[:, 6, 0:B], 1.0 / (VISION * D), 1e-8, ALU.mult, ALU.add))
                link(nc.vector.reciprocal(row(5, B), vis))
                link(nc.vector.scalar_tensor_tensor(out=ratio, in0=ps[:, 6, B:2 * B], scalar=1.0 / ((S - VISION) * D),
                                                    in1=row(5, B), op0=ALU.mult, op1=ALU.mult))
                rg = row(6, B * E).rearrange("p (b e) -> p b e", b=B)
                link(tt(rg, ratio.unsqueeze(2).broadcast_to([P, B, E]),
                        gate_v[:, D:D + 1, :].broadcast_to([P, B, E]), ALU.mult))
                link(tt(rg, rg, gate_bias[:, :].unsqueeze(1).broadcast_to([P, B, E]), ALU.add))
                lg = row(7, T * E).rearrange("p (t e) -> p t e", t=T)
                link(tt(lg.rearrange("p (b j) e -> p b j e", b=B), logits[:, :, :].rearrange("p (b j) e -> p b j e", b=B),
                        rg.unsqueeze(2).broadcast_to([P, B, TB, E]), ALU.add))
                link(nc.vector.tensor_reduce(row(8, T), lg, AX.X, ALU.max))
                tt(row(0, T * E).rearrange("p (t e) -> p t e", t=T), lg,
                   row(8, T).unsqueeze(2).broadcast_to([P, T, E]), ALU.subtract).then_inc(route.shifted.sem, 1)
                need(dve, route.exp, 0, 1)
                ex = row(10, T * E).rearrange("p (t e) -> p t e", t=T)
                link(nc.vector.tensor_reduce(row(8, T), ex, AX.X, ALU.add))
                link(nc.vector.reciprocal(row(11, T), row(8, T)))
                p = row(12, T * E).rearrange("p (t e) -> p t e", t=T)
                link(tt(p, ex, row(11, T).unsqueeze(2).broadcast_to([P, T, E]), ALU.mult))
                pf = p.rearrange("p (b j) e -> p b j e", b=B)[:, :, 0, :]
                ab, ac, bc = row(14, B), row(15, B), row(16, B)
                link(tt(ab, pf[:, :, 0], pf[:, :, 1], ALU.is_ge))
                link(tt(ac, pf[:, :, 0], pf[:, :, 2], ALU.is_ge))
                link(tt(bc, pf[:, :, 1], pf[:, :, 2], ALU.is_ge))
                rank = row(17, E * B).rearrange("p (e b) -> p e b", e=E)
                link(tt(rank[:, 0, :], ab, ac, ALU.add))
                link(ts(rank[:, 0, :], rank[:, 0, :], -1.0, 2.0, ALU.mult, ALU.add))
                link(tt(rank[:, 1, :], ab, bc, ALU.subtract))
                link(ts(rank[:, 1, :], rank[:, 1, :], 1.0, None, ALU.add))
                link(tt(rank[:, 2, :], ac, bc, ALU.add))
                sel = row(19, 2 * E * B)
                for s_ in range(2):
                    link(ts(sel[:, s_ * E * B:(s_ + 1) * E * B], row(17, E * B), float(s_), None, ALU.is_equal))
                sv = sel.rearrange("p (s e b) -> p s e b", s=2, e=E)
                link(nc.vector.scalar_tensor_tensor(out=experts[:, :, :], in0=sv[:, :, 2, :], scalar=2.0,
                                                    in1=sv[:, :, 1, :], op0=ALU.mult, op1=ALU.add))
                nc.vector.tensor_copy(row(20, T * E).bitcast(BF16)[:, 0:2 * E * B], sel).then_inc(route.rank.sem, 1)
                a, b, c = p[:, :, 0], p[:, :, 1], p[:, :, 2]
                top = row(13, 2 * T).rearrange("p (s t) -> p s t", s=2)
                link(tt(row(14, T), a, b, ALU.max))
                link(tt(row(15, T), a, b, ALU.min))
                link(tt(top[:, 0, :], row(14, T), c, ALU.max))
                link(tt(row(16, T), row(14, T), c, ALU.min))
                link(tt(top[:, 1, :], row(15, T), row(16, T), ALU.max))
                link(tt(row(17, T), top[:, 0, :], top[:, 1, :], ALU.add))
                link(ts(row(17, T), row(17, T), 1e-8, None, ALU.add))
                link(nc.vector.reciprocal(row(18, T), row(17, T)))
                link(tt(top, top, row(18, T).unsqueeze(1).broadcast_to([P, 2, T]), ALU.mult))
                need(dve, route.spread, 0, 1)
                link(nc.vector.tensor_copy(sel, ps[:, 6, 0:2 * E * B]))
                for s_ in range(2):
                    for e in range(E):
                        link(tt(coef[:, s_, :, e].rearrange("p (b j) -> p b j", b=B),
                                top[:, s_, :].rearrange("p (b j) -> p b j", b=B),
                                sv[:, s_, e, :].unsqueeze(2).broadcast_to([P, B, TB]), ALU.mult))
                link(tt(coef_b2[:, :, :], coef[:, 0, :, :], coef[:, 1, :, :], ALU.add))
                ts(coef[:, :, :, 2], coef[:, :, :, 2], 0.5, None, ALU.mult).then_inc(route.coef.sem, 1)
                need(dve, route.coef, 0, 1)

            def mix(ffn, n, i, s):
                t = index(n)
                x = ps[:, 2 * i + s, :]
                c = [coef[:, s, t, e:e + 1] for e in range(E)]
                u = funs[:, s, 2, :]
                k = 4 * s
                need(dve, ffn.fun, n, 3 * s + 3)
                nc.vector.tensor_scalar(u, u, c[2], c[2], ALU.mult, ALU.add).then_inc(ffn.mix.sem, 1)
                need(dve, ffn.mix, n, k + 1)
                nc.vector.tensor_tensor(u, x, u, ALU.mult).then_inc(ffn.mix.sem, 1)
                need(dve, ffn.mix, n, k + 2)
                nc.vector.scalar_tensor_tensor(out=u, in0=funs[:, s, 1, :], scalar=c[1], in1=u,
                                               op0=ALU.mult, op1=ALU.add).then_inc(ffn.mix.sem, 1)
                need(dve, ffn.mix, n, k + 3)
                nc.vector.scalar_tensor_tensor(out=act_tok[:, i, s, :], in0=funs[:, s, 0, :], scalar=c[0], in1=u,
                                               op0=ALU.mult, op1=ALU.add).then_inc(ffn.mix.sem, 1)

            def finish(ffn, n, after):
                need(dve, ffn.y_ps, n, 1)
                t = index(n)
                x = x_sb[:, t, :]
                nc.vector.tensor_tensor(x, ps[:, 6, :], x, ALU.add).then_inc(ffn.y_add.sem, 1)
                need(dve, ffn.y_add, n, 1)
                for e in range(E):
                    nc.vector.scalar_tensor_tensor(out=x, in0=b2_row[:, e, :], scalar=coef_b2[:, t, e:e + 1], in1=x,
                                                   op0=ALU.mult, op1=ALU.add).then_inc(ffn.b2_add.sem, 1)
                    need_apart(dve, ffn.b2_add, n, e + 1)
                if after is not None:
                    norm(after, n)

            def low_part(out, high, bank, signal):
                nc.vector.tensor_tensor(out, ps[:, bank, :].rearrange("p (c t) -> p c t", c=KC),
                                        high.bitcast(F32), ALU.subtract).then_inc(signal.sem, 1)

            def ffn_dve_step(ffn, n, i, after, back, front, mid):
                if ffn.split and back:
                    for s in range(2):
                        need(dve, ffn.aT, shift(n, -2), s + 1)
                        low_part(aT_lo[:, s], aT_hi[:, s], 4 + s, ffn.aT_low)
                if ffn.split and front:
                    need(dve, ffn.hT, n, 1)
                    low_part(hT_lo[:, i], hT_hi[:, i], 7, ffn.hT_low)
                if mid:
                    mix(ffn, shift(n, -1), 1 - i, 1)
                if back:
                    finish(ffn, shift(n, -2), after)
                if front:
                    mix(ffn, n, i, 0)

            def ffn_dve(ffn, after):
                dve.sem_inc(ffn.y_add.sem, 1)
                ffn_dve_step(ffn, 0, 0, after, False, True, False)
                ffn_dve_step(ffn, 1, 1, after, False, True, True)
                with dve.Fori(0, T // 2 - 1) as b:
                    for i in range(2):
                        ffn_dve_step(ffn, Step(b, 2, 2 + i), i, after, True, True, True)
                ffn_dve_step(ffn, T, 0, after, True, False, True)
                ffn_dve_step(ffn, T + 1, 1, after, True, False, False)

            route_dve(route1)
            ffn_dve(ffn1, norm3)

            def search(n):
                k = [0]

                def link(ins):
                    ins.then_inc(mlp.pick.sem, 1)
                    k[0] += 1
                    need(dve, mlp.pick, n, k[0])

                need_apart(dve, mlp.size, n, 1)
                link(nc.vector.tensor_scalar(guess[:, :], size_sum[:, :], FIRST_GUESS / I, None, ALU.mult))
                for probe in range(PROBES - 1):
                    link(nc.vector.tensor_scalar(mlp_flag[:, :], mlp_size[:, :], guess[:, :], None, ALU.is_ge, ALU.add,
                                                 accum_out=cut_count[:, :]))
                    link(nc.vector.tensor_scalar(guess_step[:, :], cut_count[:, :], STEP, 1.0 - STEP * AIM,
                                                 ALU.mult, ALU.add))
                    link(nc.vector.tensor_tensor(guess[:, :], guess[:, :], guess_step[:, :], ALU.mult))
                link(nc.vector.tensor_scalar(mlp_flag[:, :], mlp_size[:, :], guess[:, :], None, ALU.is_ge, ALU.add,
                                             accum_out=cut_count[:, :]))
                link(nc.vector.tensor_scalar(short[:, :], cut_count[:, :], -1.0, float(KEEP), ALU.mult, ALU.add))
                link(nc.vector.tensor_copy(ladder[:, 0:1], guess[:, :]))
                need_apart(dve, mlp.prodT_ps, shift(n, -1), 3)
                link(nc.vector.scalar_tensor_tensor(out=mlp_prod[:, :], in0=mlp_size[:, :], scalar=guess[:, :],
                                                    in1=mlp_size[:, :], op0=ALU.is_lt, op1=ALU.mult))
                need_apart(dve, mlp.pick, n, k[0])
                link(nc.vector.max(ladder[:, 1:9], mlp_prod[:, :]))
                link(nc.vector.scalar_tensor_tensor(out=mlp_prod[:, :], in0=mlp_prod[:, :], scalar=ladder[:, 8:9],
                                                    in1=mlp_prod[:, :], op0=ALU.is_lt, op1=ALU.mult))
                need_apart(dve, mlp.pick, n, k[0])
                link(nc.vector.max(ladder[:, 9:17], mlp_prod[:, :]))
                link(nc.vector.scalar_tensor_tensor(out=pickout[:, :], in0=numbers[:, :], scalar=short[:, :],
                                                    in1=ladder[:, :], op0=ALU.is_equal, op1=ALU.mult,
                                                    accum_out=threshold[:, :]))
                link(nc.vector.tensor_scalar(mlp_flag[:, :], mlp_size[:, :], threshold[:, :], None, ALU.is_ge, ALU.add,
                                             accum_out=cut_count[:, :]))
                link(nc.vector.tensor_scalar(failed[:, :], cut_count[:, :], float(KEEP), None, ALU.not_equal))
                assert k[0] == PICKS, (k[0], PICKS)

            def product(n):
                need(dve, mlp.up, n, 1)
                nc.vector.tensor_tensor(mlp_prod[:, :], mlp_s[:, :], up_ps, ALU.mult).then_inc(mlp.prod.sem, 1)
                need(dve, mlp.prod, n, 1)
                nc.vector.tensor_tensor(mlp_prod[:, :], mlp_prod[:, :], mlp_flag[:, :], ALU.mult
                                        ).then_inc(mlp.prod.sem, 1)
                need_apart(dve, mlp.check, n, 1)
                nc.vector.tensor_copy(failures[0:1, :], check_ps).then_inc(mlp.prod.sem, 1)
                need_apart(dve, mlp.prod, n, 3)
                some = dve.value_load(failures[0:1, 0:1], min_val=0, max_val=P)
                with dve.If(some > 0):
                    search_bits(n)
                with dve.Else():
                    dve.sem_inc(mlp.slow.sem, SLOW)

            def search_bits(n):
                nc.vector.memset(cut_at[:, :], 0).then_inc(mlp.slow.sem, 1)
                with dve.Fori(0, BITS) as bit:
                    def after(k):
                        dve.wait_ge(mlp.slow.sem, mlp.slow.count(n, 1) + (bit * 4 + k))

                    after(0)
                    nc.vector.tensor_tensor(cut_try[:, :], cut_at[:, :], bits[:, bass.ds(bit, 1)],
                                            ALU.bitwise_or).then_inc(mlp.slow.sem, 1)
                    after(1)
                    nc.vector.tensor_scalar(mlp_flag[:, :], mlp_size[:, :], cut_try[:, :].bitcast(F32), None,
                                            ALU.is_ge, ALU.add, accum_out=cut_count[:, :]).then_inc(mlp.slow.sem, 1)
                    after(2)
                    nc.vector.scalar_tensor_tensor(out=cut_add[:, :], in0=cut_count[:, :], scalar=float(KEEP),
                                                   in1=bits[:, bass.ds(bit, 1)], op0=ALU.is_ge,
                                                   op1=ALU.mult).then_inc(mlp.slow.sem, 1)
                    after(3)
                    nc.vector.tensor_tensor(cut_at[:, :], cut_at[:, :], cut_add[:, :],
                                            ALU.bitwise_or).then_inc(mlp.slow.sem, 1)
                k = [1 + 4 * BITS]

                def link(ins):
                    ins.then_inc(mlp.slow.sem, 1)
                    k[0] += 1
                    if k[0] < SLOW:
                        need(dve, mlp.slow, n, k[0])

                need(dve, mlp.slow, n, k[0])
                cut = cut_at[:, :].bitcast(F32)
                link(nc.vector.tensor_scalar(mlp_flag[:, :], mlp_size[:, :], cut, None,
                                             ALU.is_ge, ALU.add, accum_out=cut_count[:, :]))
                link(nc.vector.tensor_scalar(surplus[:, :], cut_count[:, :], -float(KEEP), None, ALU.add))
                link(nc.vector.tensor_scalar(mlp_flag[:, :], mlp_size[:, :], cut, None, ALU.is_equal))
                link(nc.vector.tensor_tensor_scan(mlp_prod[:, :], mlp_flag[:, :], mlp_flag[:, :], 0.0,
                                                  ALU.add, ALU.bypass))
                link(nc.vector.scalar_tensor_tensor(out=mlp_flag[:, :], in0=mlp_prod[:, :], scalar=surplus[:, :],
                                                    in1=mlp_flag[:, :], op0=ALU.is_le, op1=ALU.mult))
                link(nc.vector.scalar_tensor_tensor(out=mlp_flag[:, :], in0=mlp_size[:, :], scalar=cut,
                                                    in1=mlp_flag[:, :], op0=ALU.is_ge, op1=ALU.subtract))
                link(nc.vector.tensor_tensor(mlp_prod[:, :], mlp_s[:, :], up_ps, ALU.mult))
                link(nc.vector.tensor_tensor(mlp_prod[:, :], mlp_prod[:, :], mlp_flag[:, :], ALU.mult))
                assert k[0] == SLOW

            def mlp_add(n):
                need(dve, mlp.y_ps, n, 1)
                x = x_sb[:, index(n), :]
                nc.vector.tensor_tensor(x, ps[:, Y_BANK, :], x, ALU.add).then_inc(mlp.y_add.sem, 1)

            def mlp_finish(n):
                need_apart(dve, mlp.y_add, n, 1)
                norm(norm4, n)
                logit_rows(norm4, route2, n)

            dve.sem_inc(mlp.y_add.sem, 1)
            dve.wait_ge(bits_set, BITS + 17)

            def mlp_dve_step(n, back):
                search(n)
                if back:
                    mlp_add(shift(n, -1))
                product(n)
                if back:
                    mlp_finish(shift(n, -1))
                keep_product(n)

            def keep_product(n):
                for k in range(3):
                    need(dve, mlp.prodT_ps, n, k + 1)
                    chunks = min(4, IC - 4 * k)
                    if k == 2 and I % P:
                        chunks -= 1
                    nc.vector.tensor_copy(prodT[:, 4 * k:4 * k + chunks, :],
                                   ps[:, PROD_BANK[k], 0:chunks * P].rearrange("p (c t) -> p c t", t=P)
                                   ).then_inc(mlp.prodT.sem, 1)
                    if k == 2:
                        m = I - I // P * P
                        nc.vector.tensor_copy(prodT[0:m, IC - 1, :], ps[0:m, PROD_BANK[2], chunks * P:(chunks + 1) * P]
                                       ).then_inc(mlp.prodT.sem, 1)

            mlp_dve_step(0, False)
            with dve.Fori(0, T // 2 - 1) as b:
                for i in range(2):
                    mlp_dve_step(Step(b, 2, 1 + i), True)
            search(T - 1)
            mlp_add(T - 2)
            product(T - 1)
            keep_product(T - 1)
            mlp_finish(T - 2)
            mlp_add(T - 1)
            mlp_finish(T - 1)
            route_dve(route2)
            ffn_dve(ffn2, None)

        @block.tensor
        def _(pe):
            def turn_rows(b):
                need(pe, h_ok, b, TB)
                for j in range(TB):
                    need(pe, x_add, b - 2, j + 1)
                    for c in range(KC):
                        m = nc.tensor.transpose(work[j][:, c * P:(c + 1) * P],
                                                h_sb[:, j, c * P:(c + 1) * P], ident[:, :])
                    m.then_inc(hT_ps.sem, 1)

            def project_part(b, j, n, first=False):
                w = work[(3 * j + n) % 2]
                if j == 0 and n == 0:
                    need(pe, hT_ok, b, 1)
                elif j == 0 and n == 1:
                    need(pe, hT_ok, b, 2)
                elif (j, n) in ((0, 2), (1, 1), (1, 2)):
                    need(pe, qv_out, b, {(0, 2): 1, (1, 1): 2, (1, 2): 3}[(j, n)])
                else:
                    need(pe, k_out, b, 1)
                for c in range(KC):
                    if first:
                        pe.wait_ge(wqkv_in[c], 16)
                    nc.tensor.matmul(w, actT[:, c, j * P:(j + 1) * P], wqkv[:, c, n * D:(n + 1) * D],
                                     start=(c == 0), stop=False)
                if first:
                    pe.wait_ge(bias_cut, 6)
                nc.tensor.matmul(w, ones16[0:65, :], bias3[0:65, B_ATTN + n * D:B_ATTN + (n + 1) * D],
                                 start=False, stop=True).then_inc(qkv_ps.sem, 1)

            def turn(b, before, fs):
                for f in fs:
                    side, pair = f % 2, f // 2
                    if f == 0:
                        need(pe, qv_out, b, 3)
                        need(pe, k_out, b, 2)
                    elif f == 1:
                        need(pe, qv_out, b, 4)
                    elif f == 2:
                        need(pe, res1, b, 1)
                        need(pe, nmT_ok, before, 1)
                    else:
                        need(pe, res1, b, f - 1)
                    for i in range(2):
                        for j in range(TB):
                            m = nc.tensor.transpose(
                                work[f % 2][:, i * S + j * P:i * S + (j + 1) * P],
                                qk_tok[:, j, side * D + (2 * pair + i) * P:side * D + (2 * pair + i + 1) * P],
                                ident[:, :])
                    m.then_inc(tr_ps.sem, 1)

            def diagonal(mask, n):
                return mask[:, :].unsqueeze(1).broadcast_to([P, n, P])

            def scores(b, between):
                for g in range(NG):
                    if g % GHALF == 0:
                        need(pe, scat[g // GHALF], b, scat[g // GHALF].per)
                    sl = slot[g % 2]
                    if g >= 2:
                        need(pe, max_ok, b, 2 * (g - 1))
                    nc.tensor.matmul(sl[:, 0, :].rearrange("p (h k) -> p h k", h=G), ident16[:, :], diagonal(maskS, G),
                                     start=True, stop=False, skip_group_check=True)
                    for s in range(2):
                        nc.tensor.matmul(sl[:, 1 + s, :].rearrange("p (h k) -> p h k", h=2)[:, :, P:S], ident16[:, :],
                                         diagonal(maskS, 2), start=True, stop=False, skip_group_check=True)
                    for i in range(G):
                        h = g * G + i
                        nc.tensor.matmul(sl[:, 0, i * P:(i + 1) * P], qst[0:SROWS, h, 0:P],
                                         kst[0:SROWS, h, 0:P], start=False, stop=True, skip_group_check=True)
                        m = nc.tensor.matmul(sl[:, 1 + i // 2, (i % 2) * S:(i % 2 + 1) * S],
                                             qst[0:SROWS, h, P:S], kst[0:SROWS, h, :],
                                             start=False, stop=True, skip_group_check=True)
                    m.then_inc(s_ps.sem, 1)
                    between(g)

            def maxima(b, wait_bank):
                need(pe, nm_cut, b, 4)
                wait_bank()
                for j in range(TB):
                    m = nc.tensor.transpose(work[0].bitcast(BF16)[0:MAX_PARTS * H, j * P:(j + 1) * P],
                                            nmax_p[:, j, :, :].rearrange("p m h -> p (m h)"), ident16[:, :])
                m.then_inc(nmT_ps.sem, 1)

            def scores_t(b, g):
                sl = slot[g % 2]
                if g >= 2:
                    need(pe, exp_ok, b, g - 1)
                nc.tensor.matmul(sl[:, 0, :].rearrange("p (h k) -> p h k", h=G), ident16[:, :], diagonal(maskT, G),
                                 start=True, stop=False, skip_group_check=True)
                for s in range(2):
                    nc.tensor.matmul(sl[:, 1 + s, :].rearrange("p (h k) -> p h k", h=2)[:, :, 0:P], ident16[:, :],
                                     diagonal(maskT, 2), start=True, stop=False, skip_group_check=True)
                for i in range(G):
                    h = g * G + i
                    nc.tensor.matmul(sl[:, 0, i * P:(i + 1) * P], kst[0:MROWS, h, P:S],
                                     qst[0:MROWS, h, P:S], start=False, stop=True, skip_group_check=True)
                    m = nc.tensor.matmul(sl[:, 1 + i // 2, (i % 2) * S:(i % 2 + 1) * S],
                                         kst[0:MROWS, h, 0:P], qst[0:MROWS, h, :],
                                         start=False, stop=True, skip_group_check=True)
                m.then_inc(sT_ps.sem, 1)

            def weigh(b, g):
                need(pe, exp_ok, b, g + 1)
                w = work[g % 2]
                for i in range(G):
                    h = g * G + i
                    nc.tensor.matmul(w[32 * i:32 * i + 2 * HD, 0:S], v_ones[:, 0, h, :],
                                     probsT[:, g % 2, D + i * S:D + (i + 1) * S],
                                     start=True, stop=False, tile_position=(0, 32 * i), skip_group_check=True)
                for i in range(G):
                    h = g * G + i
                    m = nc.tensor.matmul(w[32 * i:32 * i + 2 * HD, P:S], v_ones[:, 1, h, :],
                                         probsT[:, g % 2, i * P:(i + 1) * P],
                                         start=False, stop=True, tile_position=(0, 32 * i), skip_group_check=True)
                m.then_inc(pv_ps.sem, 1)

            def back(b, g):
                need(pe, outT_ok, b, g + 1)
                for j in range(TB):
                    m = nc.tensor.transpose(work[g % 2][:, S + j * P:S + (j + 1) * P],
                                            outT[:, g % 2, j * P:(j + 1) * P], ident[:, :])
                m.then_inc(oTr_ps.sem, 1)

            def attend(b, last):
                need(pe, nm_in, b, nm_in.per)
                need(pe, v_copy, b, 1)
                for g in range(NG + 2):
                    if g < NG:
                        scores_t(b, g)
                    if 1 <= g <= NG:
                        n = g - 1
                        if n >= 2:
                            need(pe, norm_ok, b, n - 1)
                        elif last:
                            need(pe, x_add, b - 1, TB)
                        else:
                            need(pe, res1, b + 1, 4)
                        weigh(b, n)
                    if g >= 2:
                        back(b, g - 2)
                need(pe, norm_ok, b, NG)
                for j in range(TB):
                    for c in range(KC):
                        m = nc.tensor.transpose(work[j][:, c * P:(c + 1) * P], o_tok[:, j, c * P:(c + 1) * P],
                                                ident[:, :])
                    m.then_inc(oT_ps.sem, 1)
                for j in range(TB):
                    need(pe, oT_ok, b, j + 1)
                    for c in range(KC):
                        nc.tensor.matmul(work[j], actT[:, c, j * P:(j + 1) * P], wproj[:, c, :],
                                         start=(c == 0), stop=False)
                    nc.tensor.matmul(work[j], ones16[0:65, :], bias3[0:65, B_PROJ:B_PROJ + D],
                                     start=False, stop=True).then_inc(y_ps.sem, 1)

            pe.wait_ge(ident_ok, 4)
            turn_rows(0)
            for j in range(TB):
                for n in range(3):
                    project_part(0, j, n, first=(j == 0 and n == 0))
            pe.wait_ge(consts, 11)
            turn(0, -1, range(4))
            pe.wait_ge(alibi_in, 32)
            pe.wait_ge(wproj_in, 16)
            pe.wait_ge(bias_cut, 12)
            with pe.Fori(0, B - 1) as b:
                def between(g):
                    if g == 1:
                        turn_rows(b + 1)
                    elif 2 <= g <= 3 * TB:
                        project_part(b + 1, (g - 2) // 3, (g - 2) % 3)

                scores(b, between)
                turn(b + 1, b, (0,))
                project_part(b + 1, TB - 1, 2)
                maxima(b, lambda: need(pe, res1, b + 1, 1))
                turn(b + 1, b, (1, 2, 3))
                attend(b, False)
            scores(B - 1, lambda g: None)
            maxima(B - 1, lambda: need(pe, x_add, B - 2, 1))
            attend(B - 1, True)

            def route_pe(route):
                need(pe, route.mag, T - 1, 1)
                first, second = abs_sum[:, 0:T:2], abs_sum[:, 1:T:2]
                nc.tensor.matmul(ps[:, 6, 0:B], vision[:, :], first, start=True, stop=True, skip_group_check=True)
                nc.tensor.matmul(ps[:, 6, B:2 * B], text[:, :], first, start=True, stop=False, skip_group_check=True)
                nc.tensor.matmul(ps[:, 6, B:2 * B], ones32[:, :], second, start=False, stop=True,
                                 skip_group_check=True).then_inc(route.sums.sem, 1)
                need(pe, route.rank, 0, 1)
                nc.tensor.matmul(ps[:, 6, 0:2 * E * B], first_row[:, :], tiny[:, 20, :].bitcast(BF16)[:, 0:2 * E * B],
                                 start=True, stop=True).then_inc(route.spread.sem, 1)

            def ffn_pe_step(ffn, n, i, back, front, weights=lambda: None):
                m = shift(n, -2)
                if back:
                    for s in range(2):
                        need(pe, ffn.mix, m, 4 * s + 4)
                        for c in range(KC):
                            last = nc.tensor.transpose(ps[:, 4 + s, c * P:(c + 1) * P],
                                                       act_tok[:, i, s, c * P:(c + 1) * P], ident[:, :])
                        last.then_inc(ffn.aT_ps.sem, 1)
                if front:
                    need(pe, ffn.row, n, 1)
                    for c in range(KC):
                        last = nc.tensor.transpose(ps[:, 7, c * P:(c + 1) * P], h_cur[:, i, c * P:(c + 1) * P],
                                                   ident[:, :])
                    last.then_inc(ffn.hT_ps.sem, 1)
                if back:
                    e = [pe.value_load(experts[0:1, s, expert_of(m)], min_val=0, max_val=E - 1) for s in range(2)]
                    products = []
                    for s in range(2):
                        if ffn.split:
                            products += [(s, (ffn.aT, s + 1), aT_hi, w2_hi), (s, (ffn.aT, s + 1), aT_hi, w2_lo)]
                        else:
                            products.append((s, (ffn.aT, s + 1), aT, w2_sb))
                    if ffn.split:
                        products += [(s, (ffn.aT_low, s + 1), aT_lo, w2_hi) for s in range(2)]
                    need(pe, ffn.y_add, shift(m, -1), 1)
                    for k, (s, (signal, count), a, w) in enumerate(products):
                        need(pe, signal, m, count)
                        for c in range(KC):
                            last = nc.tensor.matmul(ps[:, 6, :], a[:, s, c, :], w[:, e[s], c, :],
                                                    start=(k == 0 and c == 0),
                                                    stop=(k == len(products) - 1 and c == KC - 1))
                    last.then_inc(ffn.y_ps.sem, 1)
                if front:
                    weights()
                    for s in range(2):
                        e = pe.value_load(experts[0:1, s, expert_of(n)], min_val=0, max_val=E - 1)
                        if ffn.split:
                            products = [(ffn.hT, hT_hi, w1_hi), (ffn.hT, hT_hi, w1_lo), (ffn.hT_low, hT_lo, w1_hi)]
                        else:
                            products = [(ffn.hT, hT, w1_sb)]
                        for k, (signal, a, w) in enumerate(products):
                            need(pe, signal, n, 1)
                            for c in range(KC):
                                nc.tensor.matmul(ps[:, 2 * i + s, :], a[:, i, c, :], w[:, e, c, :],
                                                 start=(k == 0 and c == 0), stop=False)
                        nc.tensor.matmul(ps[:, 2 * i + s, :], ones16[0:65, :],
                                         bias1[0:65, e, :], start=False, stop=True).then_inc(ffn.pre.sem, 1)

            def expert_of(n):
                if isinstance(n, Step):
                    b = n.var + n.add // 2
                    return bass.ds(b, 1)
                return slice(n // 2, n // 2 + 1)

            def ffn_pe(ffn, first_here, second_here, count):
                ffn_pe_step(ffn, 0, 0, False, True, lambda: pe.wait_ge(first_here, count))
                ffn_pe_step(ffn, 1, 1, False, True)
                pe.wait_ge(second_here, count)
                with pe.Fori(0, T // 2 - 1) as b:
                    for i in range(2):
                        ffn_pe_step(ffn, Step(b, 2, 2 + i), i, True, True)
                ffn_pe_step(ffn, T, 0, True, False)
                ffn_pe_step(ffn, T + 1, 1, True, False)

            route_pe(route1)
            ffn_pe(ffn1, w1_here, w2_here, 48)

            def turn_weights():
                pe.wait_ge(mlp_w_in, 64)
                for u in range(3 * IC):
                    which, c = divmod(u, IC)
                    n = min(P, I - c * P)
                    if which == 2 and c == 0:
                        pe.wait_ge(down_in, 16)
                    need(pe, mlp.kept, u - 6, 1)
                    for k in range(KC):
                        if which < 2:
                            last = nc.tensor.transpose(ps[:, u % 6, k * P:k * P + n],
                                                       (gate_raw, up_raw)[which][0:n, c, k * P:(k + 1) * P],
                                                       ident[0:n, 0:n])
                        else:
                            last = nc.tensor.transpose(ps[0:n, u % 6, k * P:(k + 1) * P],
                                                       down_raw[:, k, c * P:c * P + n], ident[:, :])
                    last.then_inc(mlp.turned.sem, 1)

            def wide(first_bank, n_hT, w, signal):
                for q in range(0, I, D):
                    m = min(D, I - q)
                    for c in range(KC):
                        last = nc.tensor.matmul(ps[:, first_bank + q // D, 0:m], hT[:, n_hT, c, :], w[:, c, q:q + m],
                                                start=(c == 0), stop=(c == KC - 1))
                last.then_inc(signal.sem, 1)

            def mlp_turn_row(n, i):
                need(pe, mlp.row, n, 1)
                for c in range(KC):
                    last = nc.tensor.transpose(ps[:, ROW_BANK, c * P:(c + 1) * P],
                                               h_cur[:, i, c * P:(c + 1) * P], ident[:, :])
                last.then_inc(mlp.hT_ps.sem, 1)

            def mlp_gate(n, i):
                need(pe, mlp.hT, n, 1)
                need(pe, mlp.silu, shift(n, -1), 1)
                wide(0, i, wgT, mlp.gate)

            def check(n):
                need(pe, mlp.pick, n, PICKS)
                need(pe, mlp.y_add, shift(n, -1), 1)
                nc.tensor.matmul(check_ps, failed[:, :], ones32[:, 0:1], start=True, stop=True,
                                 skip_group_check=True).then_inc(mlp.check.sem, 1)

            def mlp_pe_step(n, i, front, early=True):
                if front:
                    need(pe, mlp.prodT, shift(n, -1), 4)
                    mlp_turn_row(shift(n, 1), 1 - i)
                need(pe, mlp.prod, shift(n, -1), 3)
                need(pe, mlp.slow, shift(n, -1), SLOW)
                wide(3, i, wuT, mlp.up)
                if early:
                    check(n)
                if front:
                    mlp_gate(shift(n, 1), 1 - i)
                if not early:
                    check(n)
                need(pe, mlp.prod, n, 3)
                need(pe, mlp.slow, n, SLOW)
                for k in range(3):
                    if k == 0 and front:
                        need(pe, mlp.hT, shift(n, 1), 1)
                    elif k == 2:
                        need(pe, mlp.prodT, n, 1)
                    for c in range(4 * k, min(4 * k + 4, IC)):
                        m = min(P, I - c * P)
                        last = nc.tensor.transpose(ps[0:m, PROD_BANK[k], (c - 4 * k) * P:(c - 4 * k + 1) * P],
                                                   mlp_prod[:, c * P:c * P + m], ident[:, :])
                    last.then_inc(mlp.prodT_ps.sem, 1)
                for c in range(IC):
                    m = min(P, I - c * P)
                    if c == 0:
                        need(pe, mlp.prodT, n, 2)
                    elif c == 8:
                        need(pe, mlp.prodT, n, 3)
                    elif c == IC - 1:
                        need(pe, mlp.prodT, n, 4)
                    last = nc.tensor.matmul(ps[:, Y_BANK, :], prodT[0:m, c, :], wdT[0:m, c, :],
                                            start=(c == 0), stop=(c == IC - 1))
                last.then_inc(mlp.y_ps.sem, 1)

            turn_weights()
            need(pe, mlp.kept, 3 * IC - 1, 1)
            need(pe, ffn1.y_add, T - 1, 1)
            mlp_turn_row(0, 0)
            mlp_gate(0, 0)
            mlp_pe_step(0, 0, True, early=False)
            mlp_pe_step(1, 1, True)
            with pe.Fori(0, T // 2 - 2) as b:
                for i in range(2):
                    mlp_pe_step(Step(b, 2, 2 + i), i, True)
            mlp_pe_step(T - 2, 0, True)
            mlp_pe_step(T - 1, 1, False)
            route_pe(route2)
            ffn_pe(ffn2, w1_low, w2_low, E)


_INS = ["L0_attn_a_hidden_states", "L0_attn_a_w_attn", "L0_attn_a_b_attn", "L0_attn_a_w_proj", "L0_attn_a_b_proj",
        "L0_attn_b_w_gate", "L0_attn_b_w_up", "L0_attn_b_w_down", "L0_ffn_gate_w", "L0_ffn_gate_b",
        "L0_ffn_w1", "L0_ffn_b1", "L0_ffn_w2", "L0_ffn_b2"]


def kernel(**inputs):
    import concourse.bacc as bacc
    from concourse.bass_utils import run_bass_kernel_spmd

    nc = bacc.Bacc("TRN2", target_bir_lowering=False, num_devices=1)
    arrays = {f"in_{name}": np.ascontiguousarray(inputs[name]) for name in _INS}
    B, S, D = arrays["in_" + _INS[0]].shape
    arrays["k_alibi"], arrays["q_alibi"] = alibi_rows(32, S)
    args = [nc.dram_tensor(n, a.shape, mybir.dt.from_np(a.dtype), kind="ExternalInput").ap()
            for n, a in arrays.items()]
    out = nc.dram_tensor("out", (B, S, D), F32, kind="ExternalOutput").ap()
    build(nc, *args, out)
    r = run_bass_kernel_spmd(nc, [arrays], core_ids=[0])
    return r.results[0]["out"]
```
